# Optimizing a Trainium2 kernel written in Bass

```python
import numpy as np
import jax
import jax.numpy as jnp

def _softmax(x, axis=-1):
    return jax.nn.softmax(x, axis=axis)

def _gelu(x):
    return jax.nn.gelu(x, approximate=True)

def _silu(x):
    return jax.nn.silu(x)

def _sigmoid(x):
    return jax.nn.sigmoid(x)

def _layernorm(x, axis=-1, eps=1e-05):
    m = jnp.mean(x, axis=axis, keepdims=True)
    v = jnp.var(x, axis=axis, keepdims=True)
    return (x - m) / jnp.sqrt(v + eps)

def _scatter_add(tgt, idx, src, axis=0):
    return tgt.at[idx].add(src)

def _segment_sum(src, seg, n):
    return jax.ops.segment_sum(src, seg, n)
kernel_name = 'mk_cond_resid_d4_seqx_r4_e3e60c'

def setup_inputs(seed: int=0):
    np.random.seed(seed)
    _w = jnp.asarray

    def _rec_inputs():
        import jax
        import jax.numpy as jnp
        _rk = jax.random.key(seed)
        x = -0.000125 + 0.9999 * jax.random.normal(jax.random.fold_in(_rk, 1), (8, 256, 1024), jnp.float32)
        _lenS = 256 - jax.random.randint(jax.random.fold_in(_rk, 7), (8,), 0, max(1, 256 // 4) + 1, jnp.int32)
        _lenS2 = 256 - jax.random.randint(jax.random.fold_in(_rk, 8), (8,), 0, max(1, 256 // 4) + 1, jnp.int32)
        itok_B_0_4 = jax.random.randint(jax.random.fold_in(_rk, 11), (8,), 0, 5, jnp.int32)
        condB_codebook = -0.0625 + 0.715345 * jax.random.normal(jax.random.fold_in(_rk, 12), (8,), jnp.float32)
        itok_B_0_2 = jax.random.randint(jax.random.fold_in(_rk, 13), (8,), 0, 3, jnp.int32)
        itok_B_0_7 = jax.random.randint(jax.random.fold_in(_rk, 14), (8,), 0, 8, jnp.int32)
        return (x, itok_B_0_4, condB_codebook, itok_B_0_2, itok_B_0_7)
    x, itok_B_0_4, condB_codebook, itok_B_0_2, itok_B_0_7 = _rec_inputs()

    def _L0_cond_setup():
        import jax, jax.numpy as jnp
        import numpy as np
        LORA_SCALING = 16.0 / 32.0
        key = jax.random.key(seed)
        k1, k2, k3, k4, k5 = jax.random.split(key, 5)
        B, S, D, R, L = (4, 512, 1024, 32, 5)
        x = jax.random.normal(k1, (B, S, D), dtype=jnp.float32)
        weight = jax.random.normal(k2, (D, D), dtype=jnp.float32) * 0.02
        lora_A = jax.random.normal(k3, (L, D, R), dtype=jnp.float32) * 0.02
        lora_B_w = jax.random.normal(k4, (D, R), dtype=jnp.float32) * 0.02
        labeler_index = jax.random.randint(k5, (B,), 0, L, dtype=jnp.int32)
        return {'x': x, 'weight': weight, 'lora_A': lora_A, 'lora_B_w': lora_B_w, 'labeler_index': labeler_index}
    _L0_cond_all = _L0_cond_setup()
    _L0_cond_in = {k: v for k, v in _L0_cond_all.items() if k in ('weight', 'lora_A', 'lora_B_w')}
    del _L0_cond_all

    def _L1_cond_setup():
        import jax, jax.numpy as jnp
        import numpy as np
        GROUP = 128
        LORA_ALPHA = 32.0
        LORA_RANK = 64
        key = jax.random.key(seed)
        k1, k2, k3, k4 = jax.random.split(key, 4)
        O, I = (1024, 1024)
        x = jax.random.normal(k1, (4, 512, I), dtype=jnp.float32)
        weight = jax.random.normal(k2, (O, I), dtype=jnp.float32) * 0.02
        wg = weight.reshape(O, I // GROUP, GROUP)
        scale_log = jnp.log(jnp.clip(jnp.max(jnp.abs(wg), axis=2, keepdims=True), 1e-05))
        codebook = jnp.array([-1.0, -0.25, 0.0, 1.0], dtype=jnp.float32)
        lora_A = jax.random.normal(k3, (LORA_RANK, I), dtype=jnp.float32) * 0.02
        lora_B = jax.random.normal(k4, (O, LORA_RANK), dtype=jnp.float32) * 0.02
        return {'x': x, 'weight': weight, 'scale_log': scale_log, 'codebook': codebook, 'lora_A': lora_A, 'lora_B': lora_B}
    _L1_cond_all = _L1_cond_setup()
    _L1_cond_in = {k: v for k, v in _L1_cond_all.items() if k in ('weight', 'scale_log', 'lora_A', 'lora_B')}
    del _L1_cond_all

    def _L2_cond_setup():
        import jax, jax.numpy as jnp
        import numpy as np
        B, S, D_IN, D_OUT = (4, 512, 1024, 1024)
        R, NUM_LABELERS = (32, 5)
        LORA_SCALING = 16 / 32
        key = jax.random.key(seed)
        k1, k2, k3, k4, k5 = jax.random.split(key, 5)
        x = jax.random.normal(k1, (B, S, D_IN), dtype=jnp.float32)
        labeler_index = jax.random.randint(k2, (B,), 0, NUM_LABELERS, dtype=jnp.int64)
        W = jax.random.normal(k3, (D_OUT, D_IN), dtype=jnp.float32) * 0.02
        lora_A = jax.random.normal(k4, (NUM_LABELERS, D_IN, R), dtype=jnp.float32) * 0.02
        lora_B_w = jax.random.normal(k5, (D_OUT, R), dtype=jnp.float32) * 0.02
        return {'x': x, 'labeler_index': labeler_index, 'W': W, 'lora_A': lora_A, 'lora_B_w': lora_B_w}
    _L2_cond_all = _L2_cond_setup()
    _L2_cond_in = {k: v for k, v in _L2_cond_all.items() if k in ('W', 'lora_A', 'lora_B_w')}
    del _L2_cond_all

    def _L3_cond_setup():
        import jax, jax.numpy as jnp
        import numpy as np
        TOP_K = 2
        LANG_BIAS = 5.0
        SCALING = 32.0 / 16.0
        LANGUAGE_PAD_ID = -1
        key = jax.random.key(seed)
        ks = jax.random.split(key, 6)
        B, T, D, O, E, R = (4, 512, 1024, 1024, 8, 16)
        x = jax.random.normal(ks[0], (B, T, D), dtype=jnp.float32)
        language_ids = jax.random.randint(ks[1], (B,), 0, E).astype(jnp.int64)
        W = jax.random.normal(ks[2], (O, D), dtype=jnp.float32) * (1.0 / np.sqrt(D))
        Wr = jax.random.normal(ks[3], (E, D), dtype=jnp.float32) * (1.0 / np.sqrt(D))
        A = jax.random.normal(ks[4], (E, R, D), dtype=jnp.float32) * (1.0 / np.sqrt(D))
        Bm = jax.random.normal(ks[5], (O, R), dtype=jnp.float32) * 0.0
        Bm = jnp.broadcast_to(Bm, (E, O, R)) + jax.random.normal(ks[5], (E, O, R), dtype=jnp.float32) * 0.02
        return {'x': x, 'language_ids': language_ids, 'W': W, 'Wr': Wr, 'A': A, 'B': Bm}
    _L3_cond_all = _L3_cond_setup()
    _L3_cond_in = {k: v for k, v in _L3_cond_all.items() if k in ('W', 'Wr', 'A', 'B')}
    del _L3_cond_all
    return {'x': x, 'itok_B_0_4': itok_B_0_4, 'condB_codebook': condB_codebook, 'itok_B_0_2': itok_B_0_2, 'itok_B_0_7': itok_B_0_7, 'L0_cond_weight': _L0_cond_in['weight'], 'L0_cond_lora_A': _L0_cond_in['lora_A'], 'L0_cond_lora_B_w': _L0_cond_in['lora_B_w'], 'L1_cond_weight': _L1_cond_in['weight'], 'L1_cond_scale_log': _L1_cond_in['scale_log'], 'L1_cond_lora_A': _L1_cond_in['lora_A'], 'L1_cond_lora_B': _L1_cond_in['lora_B'], 'L2_cond_W': _L2_cond_in['W'], 'L2_cond_lora_A': _L2_cond_in['lora_A'], 'L2_cond_lora_B_w': _L2_cond_in['lora_B_w'], 'L3_cond_W': _L3_cond_in['W'], 'L3_cond_Wr': _L3_cond_in['Wr'], 'L3_cond_A': _L3_cond_in['A'], 'L3_cond_B': _L3_cond_in['B']}

def reference(x, itok_B_0_4, condB_codebook, itok_B_0_2, itok_B_0_7, L0_cond_weight, L0_cond_lora_A, L0_cond_lora_B_w, L1_cond_weight, L1_cond_scale_log, L1_cond_lora_A, L1_cond_lora_B, L2_cond_W, L2_cond_lora_A, L2_cond_lora_B_w, L3_cond_W, L3_cond_Wr, L3_cond_A, L3_cond_B):
    import jax
    import jax.numpy as jnp

    def _L0_cond_ref(x, weight, lora_A, lora_B_w, labeler_index):
        import jax, jax.numpy as jnp
        import numpy as np
        LORA_SCALING = 16.0 / 32.0
        result = jnp.einsum('bsd,od->bso', x, weight)
        labelers_A = lora_A[labeler_index]
        low = jnp.einsum('bsd,bdr->bsr', x, labelers_A)
        result = result + jnp.einsum('bsr,or->bso', low, lora_B_w) * LORA_SCALING
        return result

    def _L1_cond_ref(x, weight, scale_log, codebook, lora_A, lora_B):
        import jax, jax.numpy as jnp
        import numpy as np
        GROUP = 128
        LORA_ALPHA = 32.0
        LORA_RANK = 64
        O, I = weight.shape
        lora_delta = lora_B @ lora_A * (LORA_ALPHA / LORA_RANK)
        cb = codebook / jnp.clip(jnp.max(jnp.abs(codebook)), 1e-08)
        scale = jnp.exp(scale_log)
        wg = (weight + lora_delta).reshape(O, I // GROUP, GROUP)
        normalized = wg / scale
        thresholds = (cb[:-1] + cb[1:]) * 0.5
        idx = jnp.searchsorted(thresholds, normalized, side='left')
        quantized = cb[idx]
        w = jax.lax.stop_gradient(quantized - normalized) + normalized
        w_q = (w * scale).reshape(O, I)
        w_eff = w_q + lora_delta
        return x @ w_eff.T

    def _L2_cond_ref(x, labeler_index, W, lora_A, lora_B_w):
        import jax, jax.numpy as jnp
        import numpy as np
        B, S, D_IN, D_OUT = (4, 512, 1024, 1024)
        R, NUM_LABELERS = (32, 5)
        LORA_SCALING = 16 / 32
        base = jnp.einsum('bsi,oi->bso', x, W)
        labelers_A = lora_A[labeler_index]
        low = jnp.einsum('bsi,bir->bsr', x, labelers_A)
        delta = jnp.einsum('bsr,or->bso', low, lora_B_w) * LORA_SCALING
        return base + delta

    def _L3_cond_ref(x, language_ids, W, Wr, A, B):
        import jax, jax.numpy as jnp
        import numpy as np
        TOP_K = 2
        LANG_BIAS = 5.0
        SCALING = 32.0 / 16.0
        LANGUAGE_PAD_ID = -1
        base = jnp.einsum('btd,od->bto', x, W)
        E = Wr.shape[0]
        logits = jnp.einsum('btd,ed->bte', x.astype(jnp.float32), Wr.astype(jnp.float32))
        expert_targets = language_ids
        valid = expert_targets >= 0
        tgt = jnp.where(valid, expert_targets, 0)
        bias = jax.nn.one_hot(tgt, E, dtype=logits.dtype) * LANG_BIAS
        bias = jnp.where(valid[:, None], bias, 0.0)
        logits = logits + bias[:, None, :]
        topw, topi = jax.lax.top_k(logits, TOP_K)
        weights = jax.nn.softmax(topw, axis=-1)
        gates = jnp.sum(jax.nn.one_hot(topi, E, dtype=weights.dtype) * weights[..., None], axis=-2)
        gates = gates.astype(x.dtype)
        h = jnp.einsum('btd,erd->bter', x, A)
        lora_out = jnp.einsum('bter,bte,eor->bto', h, gates, B)
        return base + SCALING * lora_out
    x = x + _L0_cond_ref(x, L0_cond_weight, L0_cond_lora_A, L0_cond_lora_B_w, itok_B_0_4)
    x = x + _L1_cond_ref(x, L1_cond_weight, L1_cond_scale_log, condB_codebook, L1_cond_lora_A, L1_cond_lora_B)
    x = x + _L2_cond_ref(x, itok_B_0_2, L2_cond_W, L2_cond_lora_A, L2_cond_lora_B_w)
    x = x + _L3_cond_ref(x, itok_B_0_7, L3_cond_W, L3_cond_Wr, L3_cond_A, L3_cond_B)
    return x

_drawn_inputs = setup_inputs


def setup_inputs(seed=0):
    import zlib

    import numpy as np

    out = dict(_drawn_inputs(seed))
    spreads = {}
    factors = {}
    for name, (base, spread) in spreads.items():
        noise = np.random.default_rng([zlib.crc32(name.encode()), seed]).standard_normal(out[name].shape)
        drawn = base * np.exp(spread * noise) if base else spread * noise
        out[name] = jnp.asarray(drawn.astype(out[name].dtype))
    for name, factor in factors.items():
        out[name] = (out[name] * factor).astype(out[name].dtype)
    return out
```

```python
from contextlib import ExitStack
from math import factorial

import concourse.bass as bass
from concourse import mybir

ALU = mybir.AluOpType
ACT = mybir.ActivationFunctionType
AX = mybir.AxisListType
F32 = mybir.dt.float32
F32R = mybir.dt.float32r
I32 = mybir.dt.int32
U32 = mybir.dt.uint32

P = 128
LOG2E = 1.4426950408889634
LN2_HIGH = 0.693359375
LN2_LOW = -2.12194440054690583e-4
ROUND = 1.5 * (1 << 23)
EXP_TERMS = 8
EXP_LOW, EXP_HIGH = -87.0, 88.0
BANK = 512


class Chain:

    def __init__(self, eng, sem):
        self.eng, self.sem, self.n = eng, sem, 0

    def __call__(self, instruction):
        instruction.then_inc(self.sem, 1)
        self.n = self.n + 1
        self.eng.wait_ge(self.sem, self.n)


def build(nc, x, lab0, codebook, lab2, lab7, W0, A0, B0, W1, scale_log, A1, B1, W2, A2, B2, W3, Wr, A3, B3, out):
    BATCH, SEQ, D = x.shape
    LABELS, _, R = A0.shape
    R1 = A1.shape[0]
    E, RE, _ = A3.shape
    ER = E * RE
    KT = D // P
    G1 = scale_log.shape[1]
    LEVELS = codebook.shape[0]
    TILES = BATCH * SEQ // P
    PER_BATCH = SEQ // P
    C_H, C_LOGIT, C_LOW2 = D, D + ER, D + ER + E
    C_ALL = C_LOW2 + LABELS * R
    NR = ER + E
    assert (D, PER_BATCH, D // G1, ER, KT, LEVELS, R1, R) == (1024, 2, P, P, 8, 8, 64, 32)
    W_IN = (C_LOW2, C_ALL, C_ALL)
    STEP0 = (0, KT + 1, 2 * KT + 1)
    PASSES = 3 * KT + 2
    HALF = KT // 2

    def chunks(width):
        return [(c, min(width, c + BANK)) for c in range(0, width, BANK)]

    with ExitStack() as ctx:
        def sb(name, shape, dt=F32, stack=ctx):
            return stack.enter_context(nc.sbuf_tensor(name, shape, dt))

        def sem(name):
            return ctx.enter_context(nc.semaphore(name))

        h_hi = sb("h_hi", [P, KT, C_ALL], F32R)
        h_lo = sb("h_lo", [P, KT, C_ALL], F32R)
        ident = sb("ident", [P, P])
        bp = sb("bp", [2 * R, C_ALL])
        b2raw, b0raw = sb("b2raw", [P, KT, R]), sb("b0raw", [P, KT, R])
        b2h, b2l = sb("b2h", [P, KT, R], F32R), sb("b2l", [P, KT, R], F32R)
        b0h, b0l = sb("b0h", [P, KT, R], F32R), sb("b0l", [P, KT, R], F32R)
        scale, rscale = sb("scale", [P, KT, G1]), sb("rscale", [P, KT, G1])
        exp_t, exp_n = sb("exp_t", [P, 2, KT, G1]), sb("exp_n", [P, KT, G1], I32)
        book = sb("book", [P, LEVELS])
        steps = sb("steps", [P, LEVELS])
        thr = sb("thr", [P, LEVELS])
        tmp8 = sb("tmp8", [P, 2 * LEVELS])
        labi = sb("labi", [1, 2 * BATCH], I32)
        labf = sb("labf", [1, 4 * BATCH])
        labu = sb("labu", [1, 2 * BATCH], I32)
        lab7i = sb("lab7i", [P, BATCH], I32)
        lab7f = sb("lab7f", [P, BATCH])
        iota_i = sb("iota_i", [P, E], I32)
        iota_f = sb("iota_f", [P, E])
        bias7 = sb("bias7", [P, BATCH, E])

        first = ExitStack()
        g = sb("g", [P, KT, C_ALL], F32, first)
        w1_st = sb("w1_st", [P, 2, KT, P], F32, first)
        w1_eff = sb("w1_eff", [P, HALF, KT, P], F32, first)
        ldelta = sb("ldelta", [P, KT, P], F32, first)
        qtmp = sb("qtmp", [P, KT, P], F32, first)
        a1 = sb("a1", [R1, D], F32, first)
        b1t = sb("b1t", [R1, D], F32, first)
        w_hi = sb("w_hi", [P, 2, KT, P], F32R, first)
        w_lo = sb("w_lo", [P, 2, KT, P], F32R, first)
        w_st = sb("w_st", [P, 2, KT, P], F32, first)
        first.close()
        second = ctx
        vb_hi, vb_lo = sb("vb_hi", [2 * R, C_LOW2], F32R), sb("vb_lo", [2 * R, C_LOW2], F32R)
        c_hi, c_lo = sb("c_hi", [R, LABELS * R], F32R), sb("c_lo", [R, LABELS * R], F32R)
        tsel_h, tsel_l = sb("tsel_h", [2 * R, 2, P], F32R), sb("tsel_l", [2 * R, 2, P], F32R)
        out_sb = sb("out_sb", [P, 2, D])
        v_sb = sb("v_sb", [P, P])
        vt_h, vt_l = sb("vt_h", [2 * R, P], F32R), sb("vt_l", [2 * R, P], F32R)
        vm_h, vm_l = sb("vm_h", [2 * R, P], F32R), sb("vm_l", [2 * R, P], F32R)
        hg = sb("hg", [P, E, RE])
        hgt_h, hgt_l = sb("hgt_h", [P, P], F32R), sb("hgt_l", [P, P], F32R)
        gate = sb("gate", [P, 96])
        top_i = sb("top_i", [P, 8], U32)
        used = 2 * C_LOW2 + 2 * LABELS * R + 4 * P + 2 * D + P + 4 * P + P + 2 * P + 96 + 8
        sb("pad", [P, KT * C_ALL - used])
        a0_raw = sb("a0_raw", [P, KT, LABELS * R])
        a0_hi, a0_lo = sb("a0_hi", [P, KT, LABELS * R], F32R), sb("a0_lo", [P, KT, LABELS * R], F32R)
        b3_raw = sb("b3_raw", [P, KT, E, RE])
        b3_hi, b3_lo = sb("b3_hi", [P, D], F32R), sb("b3_lo", [P, D], F32R)
        sel_hi, sel_lo = sb("sel_hi", [P, 2, KT, 2 * R], F32R), sb("sel_lo", [P, 2, KT, 2 * R], F32R)
        sb("pad2", [P, 10 * D - 3 * KT * LABELS * R - 3 * D - 4 * KT * 2 * R])
        xt_hi, xt_lo = sb("xt_hi", [P, 2, KT, P], F32R), sb("xt_lo", [P, 2, KT, P], F32R)
        x_st = sb("x_st", [P, 2, D])

        acc = ctx.enter_context(nc.psum_tensor("acc", [P, 2, 3 * BANK], F32))
        aux = ctx.enter_context(nc.psum_tensor("aux", [P, 2 * BANK], F32))
        V0 = D + NR

        w3_in = [sem(f"w3_in{k}") for k in range(KT)]
        small_in, bank_in, a3_in, a2_in = sem("small_in"), sem("book_in"), sem("a3_in"), sem("a2_in")
        w_in = [sem(f"w_in{i}") for i in range(2)]
        w1_in = [sem(f"w1_in{i}") for i in range(2)]
        a0_in, b3_in = sem("a0_in"), sem("b3_in")
        x_in = [sem(f"x_in{i}") for i in range(2)]
        out_done = [sem(f"out_done{i}") for i in range(2)]
        made = sem("made")
        w3_eye = sem("w3_eye")
        w3_t = sem("w3_t")
        split_hi = sem("split_hi")
        h_ready = sem("h_ready")
        h_used = sem("h_used")
        acc_done = sem("acc_done")
        acc_free = sem("acc_free")
        w_eye = sem("w_eye")
        w_hi_done = sem("w_hi_done")
        w_split = sem("w_split")
        b_hi, b_split = sem("b_hi"), sem("b_split")
        b1_t = sem("b1_t")
        tables = sem("tables")
        ld_done, aux_free = sem("ld_done"), sem("aux_free")
        v_ready, n_ready = sem("v_ready"), sem("n_ready")
        q_ready, q_sum, w1e_done = sem("q_ready"), sem("q_sum"), sem("w1e_done")
        dve_chain = sem("dve_chain")
        a0_hd, a0_done = sem("a0_hd"), sem("a0_done")
        b3_t, b3_hd, b3_done = sem("b3_t"), sem("b3_hd"), sem("b3_done")
        vb_hd, vb_done = sem("vb_hd"), sem("vb_done")
        zeroed = sem("zeroed")
        x_tr, x_hd, x_split = sem("x_tr"), sem("x_hd"), sem("x_split")
        sel_ready = sem("sel_ready")
        main_done = sem("main_done")
        v_out, v_tr, v_hd, v_split = sem("v_out"), sem("v_tr"), sem("v_hd"), sem("v_split")
        mix_done, m_hd, m_split = sem("mix_done"), sem("m_hd"), sem("m_split")
        logits_seen = sem("logits_seen")
        r_done, d_ready, e_ready = sem("r_done"), sem("d_ready"), sem("e_ready")
        hg_ready, g_tr, g_hd, g_split = sem("hg_ready"), sem("g_tr"), sem("g_hd"), sem("g_split")
        o_done, o_act, o_dve = sem("o_done"), sem("o_act"), sem("o_dve")

        GLINKS = 10
        SELS = 6

        x_rows = x.rearrange("b s d -> (b s) d")
        out_rows = out.rearrange("b s d -> (b s) d")

        def slices(w):
            return w.rearrange("(k p) i -> p k i", p=P)

        def wait_tile_used(eng, j, k):
            last = STEP0[j] + KT - 1 + (j != 1)
            if k < KT - 1:
                eng.wait_ge(h_used, (KT - 1) * last + k + 1)
            else:
                eng.wait_ge(acc_done, last + 1)

        def tile_schedule(eng, tile):
            tile(0, 0, 0, False, True)
            tile(1, 0, 1, True, True)
            with eng.Fori(1, BATCH - 1) as b:
                for h in range(2):
                    tile(b * 2 + h, b, h, True, True)
            tile(TILES - 2, BATCH - 1, 0, True, True)
            tile(TILES - 1, BATCH - 1, 1, True, False)
            tile(TILES, BATCH, 0, True, None)

        block = ctx.enter_context(nc.Block())

        @block.sync
        def _(sp):
            for h in range(2):
                sp.sem_inc(out_done[h], 16)
            for k in range(KT):
                sp.dma_start(g[:, :, k * P:(k + 1) * P], slices(W3)[:, :, k * P:(k + 1) * P]).then_inc(w3_in[k], 16)
                if k == 0:
                    sp.dma_start(w1_eff[:, 0].rearrange("p k i -> p (k i)"),
                                 A3.rearrange("e r d -> (e r) d")).then_inc(a3_in, 16)
                    sp.dma_start(w1_eff[0:E, 1].rearrange("p k i -> p (k i)"), Wr).then_inc(a3_in, 16)
            for u in range(2):
                sp.dma_start(w_st[:, u], slices(W2)[:, :, u * P:(u + 1) * P]).then_inc(w_in[u], 16)
            sp.dma_start(book[:], codebook.rearrange("(a c) -> a c", a=1).to_broadcast([P, LEVELS])).then_inc(bank_in, 16)
            sp.dma_start(scale[:], scale_log.rearrange("(k p) g a -> p k (g a)", p=P)).then_inc(bank_in, 16)
            sp.dma_start(w1_eff[:, 2, 0:HALF].rearrange("p k i -> p (k i)").rearrange("p (k r) -> p k r", r=R1),
                         B1.rearrange("(k p) r -> p k r", p=P)).then_inc(bank_in, 16)
            sp.dma_start(a1[:], A1).then_inc(bank_in, 16)
            for m in range(2):
                sp.dma_start(w1_st[:, m], slices(W1)[:, :, m * P:(m + 1) * P]).then_inc(w1_in[m], 16)
            sp.dma_start(labi[0:1, 0:BATCH], lab0.rearrange("(a c) -> a c", a=1)).then_inc(small_in, 16)
            sp.dma_start(labi[0:1, BATCH:], lab2.rearrange("(a c) -> a c", a=1)).then_inc(small_in, 16)
            sp.dma_start(lab7i[:], lab7.rearrange("(a c) -> a c", a=1).to_broadcast([P, BATCH])).then_inc(small_in, 16)
            sp.dma_start(b2raw[:], B2.rearrange("(k p) r -> p k r", p=P)).then_inc(small_in, 16)
            sp.dma_start(b0raw[:], B0.rearrange("(k p) r -> p k r", p=P)).then_inc(small_in, 16)
            for l in range(LABELS):
                sp.dma_start(g[:, :, C_LOW2 + l * R:C_LOW2 + (l + 1) * R],
                             A2[l].rearrange("(k p) r -> p k r", p=P)).then_inc(a2_in, 16)

            def load_w(W, i, h, cols, need):
                sp.wait_ge(w_split, need)
                sp.dma_start(w_st[:, h], slices(W)[:, :, cols]).then_inc(w_in[h], 16)

            def load_w1(h, cols, need):
                sp.wait_ge(q_ready, need)
                sp.dma_start(w1_st[:, h], slices(W1)[:, :, cols]).then_inc(w1_in[h], 16)

            for h in range(2):
                load_w(W2, 1, h, bass.ds((2 + h) * P, P), h + 1)
            with sp.Fori(0, HALF // 2) as i:
                for h in range(2):
                    m = i * 2 + h
                    load_w1(h, bass.ds(m * P + 2 * P, P), m + 1)
                    load_w(W2, i, h, bass.ds(m * P + 4 * P, P), m + 3)
            for h in range(2):
                load_w(W0, 0, h, bass.ds(h * P, P), KT - 1 + h)
            for h in range(2):
                load_w1(h, bass.ds((6 + h) * P, P), 5 + h)
            sp.wait_ge(w_split, 2 * KT)
            for l in range(LABELS):
                sp.dma_start(a0_raw[:, :, l * R:(l + 1) * R], A0[l].rearrange("(k p) r -> p k r", p=P)).then_inc(a0_in, 16)
            for e in range(E):
                sp.dma_start(b3_raw[:, :, e], B3[e].rearrange("(k p) r -> p k r", p=P)).then_inc(b3_in, 16)
            with sp.Fori(0, KT // 2 - 1) as i:
                for h in range(2):
                    m = i * 2 + h
                    load_w(W0, i, h, bass.ds(m * P + 2 * P, P), m + 2 * KT + 1)

            sp.wait_ge(w_split, 3 * KT)
            for t in range(2):
                sp.dma_start(x_st[:, t], x_rows[t * P:(t + 1) * P, :]).then_inc(x_in[t], 16)

            def tile_io(t, h, load, store):
                if load:
                    sp.wait_ge(x_tr, t * 2 + 2)
                    sp.dma_start(x_st[:, h], x_rows[bass.ds(t * P + 2 * P, P), :]).then_inc(x_in[h], 16)
                if store:
                    sp.wait_ge(o_act, t + 1)
                    sp.wait_ge(o_dve, t + 1)
                    sp.dma_start(out_rows[bass.ds(t * P, P), :], out_sb[:, h]).then_inc(out_done[h], 16)

            tile_io(0, 0, True, False)
            tile_io(1, 1, True, False)
            with sp.Fori(0, TILES // 2 - 2) as i:
                for h in range(2):
                    t = i * 2 + h
                    tile_io(t + 2, h, True, False)
                    tile_io(t, h, False, True)
            for t in range(TILES - 4, TILES):
                tile_io(t, t % 2, False, True)
            for h in range(2):
                sp.wait_ge(out_done[h], 16 * (TILES // 2 + 1))

        @block.gpsimd
        def _(pool):
            def add_eye(tile, m):
                return pool.tensor_tensor(tile[:, m, :], tile[:, m, :], ident[:], ALU.add)

            pool.sem_inc(q_sum, 1)
            pool.memset(ident[:], 0.0).then_inc(made, 1)
            pool.wait_ge(made, 1)
            pool.affine_select(out=ident[:], in_=ident[:], compare_op=ALU.not_equal, fill=1.0, base=0,
                               pattern=[[-1, P]], channel_multiplier=1).then_inc(made, 1)
            pool.iota(iota_i[:], pattern=[[1, E]], base=0, channel_multiplier=0).then_inc(made, 1)
            pool.wait_ge(made, 3)
            for k in range(KT):
                pool.wait_ge(w3_in[k], 16)
                add_eye(g[:, :, k * P:(k + 1) * P], k).then_inc(w3_eye, 1)

            def eye_w(h, m, load):
                pool.wait_ge(w_in[h], 16 * load)
                add_eye(w_st[:, h], m).then_inc(w_eye, 1)

            def quant_in(m, h, load, sl):
                pool.wait_ge(w1_in[h], 16 * load)
                pool.wait_ge(aux_free, m + 2)
                pool.tensor_tensor(w1_st[:, h], w1_st[:, h], ldelta[:], ALU.add).then_inc(v_ready, 1)
                pool.wait_ge(v_ready, m + 1)
                pool.wait_ge(tables, 1)
                pool.tensor_tensor(w1_st[:, h], w1_st[:, h], rscale[:, :, bass.ds(m, 1)].to_broadcast([P, KT, P]),
                                   ALU.mult).then_inc(n_ready, 1)

            def quant_out(m, slot):
                pool.wait_ge(q_ready, m + 1)
                pool.tensor_tensor(w1_eff[:, slot], w1_eff[:, slot], ldelta[:], ALU.add).then_inc(q_sum, 1)
                pool.wait_ge(q_sum, m + 2)
                add_eye(w1_eff[:, slot], m).then_inc(w1e_done, 1)

            for h in range(2):
                eye_w(h, h, 1)
            with pool.Fori(0, HALF // 2) as i:
                for h in range(2):
                    m = i * 2 + h
                    quant_in(m, h, i + 1, m)
                    eye_w(h, m + 2, i + 2)
                    quant_out(m, m)
            for m in range(HALF, KT):
                eye_w(m % 2, (m + 2) % KT, m // 2 + 2)
            with pool.Fori(0, HALF // 2) as i:
                for h in range(2):
                    m = i * 2 + h
                    quant_in(m + HALF, h, i + 1 + HALF // 2, m)
                    quant_out(m + HALF, m)
            for m in range(2, KT):
                eye_w(m % 2, m, KT // 2 + m // 2 + 1)

            pool.wait_ge(h_ready, 4 * KT)
            pool.memset(v_sb[:], 0.0).then_inc(zeroed, 1)
            pool.memset(tsel_h[:].bitcast(F32), 0.0).then_inc(zeroed, 1)
            pool.memset(tsel_l[:].bitcast(F32), 0.0).then_inc(zeroed, 1)
            pool.wait_ge(zeroed, 3)
            for s in range(2):
                pool.tensor_copy(tsel_h[:, s, 0:2 * R], ident[0:2 * R, 0:2 * R]).then_inc(zeroed, 1)
            pool.wait_ge(zeroed, 5)
            pool.wait_ge(a0_done, 1)
            pool.wait_ge(vb_done, 2)

            def select(t, b, h, first_use):
                l0 = pool.value_load(labu[0:1, bass.ds(b, 1)], min_val=0, max_val=LABELS - 1)
                l2 = pool.value_load(labu[0:1, bass.ds(b + BATCH, 1)], min_val=0, max_val=LABELS - 1)
                if not first_use:
                    pool.wait_ge(main_done, t - 1)
                    pool.wait_ge(mix_done, t - 1)
                for dst, src in ((tsel_h[0:R, h, R:2 * R], c_hi[:, bass.ds(l2 * R, R)]),
                                 (tsel_l[0:R, h, R:2 * R], c_lo[:, bass.ds(l2 * R, R)]),
                                 (sel_hi[:, h, :, 0:R], a0_hi[:, :, bass.ds(l0 * R, R)]),
                                 (sel_lo[:, h, :, 0:R], a0_lo[:, :, bass.ds(l0 * R, R)]),
                                 (sel_hi[:, h, :, R:2 * R], h_hi[:, :, bass.ds(l2 * R + C_LOW2, R)]),
                                 (sel_lo[:, h, :, R:2 * R], h_lo[:, :, bass.ds(l2 * R + C_LOW2, R)])):
                    pool.tensor_copy(dst, src).then_inc(sel_ready, 1)

            for h in range(2):
                select(h, 0, h, True)
            with pool.Fori(1, BATCH) as b:
                for h in range(2):
                    select(b * 2 + h, b, h, False)

        @block.scalar
        def _(act):
            act.sem_inc(acc_free, 2)
            act.wait_ge(small_in, 80)
            act.mul(b2h[:], b2raw[:], 0.5).then_inc(b_hi, 1)
            act.mul(b0h[:], b0raw[:], 0.5).then_inc(b_hi, 1)
            for k in range(KT):
                act.wait_ge(w3_t, k + 1)
                act.copy(h_hi[:, k, 0:C_LOW2], acc[:, k % 2, 0:C_LOW2]).then_inc(split_hi, 1)
            act.wait_ge(b1_t, 1)
            act.mul(b1t[:], aux[0:R1, :], 0.5).then_inc(aux_free, 1)

            def high(src, s, h, ready, count):
                act.wait_ge(ready, count)
                act.copy(w_hi[:, h], src).then_inc(w_hi_done, 1)

            def copy_delta(m):
                act.wait_ge(ld_done, m + 1)
                act.wait_ge(q_sum, m + 1)
                act.copy(ldelta[:], aux[:, :].rearrange("p (k i) -> p k i", k=KT)).then_inc(aux_free, 1)

            def evacuate(j, m, slot):
                act.copy(g[:, m, 0:W_IN[j]], acc[:, slot, 0:W_IN[j]]).then_inc(acc_free, 1)

            def turn(j):
                act.wait_ge(acc_free, 2 + STEP0[j] + KT)
                if j == 0:
                    act.wait_ge(a2_in, 16 * LABELS)
                for k in range(KT):
                    wait_tile_used(act, j, k)
                    act.copy(h_hi[:, k, :], g[:, k, :]).then_inc(split_hi, 1)

            high(w_st[:, 0], 0, 0, w_eye, 1)
            high(w_st[:, 1], 1, 1, w_eye, 2)

            def step(j, m, h, src, ready, count, delta=None):
                if delta is not None:
                    copy_delta(delta)
                act.wait_ge(acc_done, m + (STEP0[j] + 1))
                if src is not None:
                    high(src, None, h, ready, count)
                evacuate(j, m, (STEP0[j] + h) % 2)

            with act.Fori(0, HALF // 2) as i:
                for h in range(2):
                    m = i * 2 + h
                    step(0, m, h, w_st[:, h], w_eye, m + 3, delta=m)
            for m in (4, 5):
                step(0, m, m % 2, w_st[:, m % 2], w_eye, m + 3)
            for m in (6, 7):
                step(0, m, m % 2, w1_eff[:, m - 6], w1e_done, m - 5)
            turn(0)
            act.wait_ge(acc_done, KT + 1)
            act.copy(bp[R:2 * R, 0:C_LOW2], acc[0:R, 0, 0:C_LOW2]).then_inc(acc_free, 1)
            with act.Fori(0, HALF // 2) as i:
                for h in range(2):
                    m = i * 2 + h
                    step(1, m, h, w1_eff[:, i * (-2) + (2 + h)], w1e_done, m + 3, delta=m + HALF)
            for m in (4, 5):
                step(1, m, m % 2, w1_eff[:, m - 2], w1e_done, m + 3)
            for m in (6, 7):
                step(1, m, m % 2, w_st[:, m % 2], w_eye, KT + m - 5)
            turn(1)
            act.wait_ge(a0_in, 16 * LABELS)
            act.copy(a0_hi[:], a0_raw[:]).then_inc(a0_hd, 1)
            with act.Fori(0, KT // 2 - 1) as i:
                for h in range(2):
                    m = i * 2 + h
                    step(2, m, h, w_st[:, h], w_eye, m + (KT + 3))
            act.wait_ge(b3_t, 1)
            act.copy(b3_hi[:], aux[:, :]).then_inc(b3_hd, 1)
            for m in (6, 7):
                step(2, m, m % 2, None, None, None)

            def x_high(t, h, half):
                act.wait_ge(x_tr, t * 2 + (half + 1))
                act.copy(xt_hi[:, h, half * HALF:(half + 1) * HALF, :],
                         aux[:, 0:BANK].rearrange("p (k i) -> p k i", k=HALF)).then_inc(x_hd, 1)

            x_high(0, 0, 0)
            turn(2)
            act.wait_ge(acc_done, PASSES)
            act.copy(bp[0:R, :], acc[0:R, 1, 0:C_ALL]).then_inc(acc_free, 1)
            act.wait_ge(acc_free, 2 + PASSES)
            act.wait_ge(h_ready, 4 * KT)
            act.copy(c_hi[:], bp[0:R, C_LOW2:C_ALL]).then_inc(vb_hd, 1)
            act.copy(vb_hi[:], bp[:, 0:C_LOW2]).then_inc(vb_hd, 1)
            x_high(0, 0, 1)

            def tile(t, b, h, finish, ahead):
                if finish:
                    act.wait_ge(v_tr, t)
                    act.copy(vt_h[:], aux[0:2 * R, BANK:BANK + P]).then_inc(v_hd, 1)
                if ahead:
                    if finish:
                        act.wait_ge(main_done, t)
                    x_high(t + 1, 1 - h, 0)
                if finish:
                    act.wait_ge(mix_done, t)
                    act.copy(vm_h[:], aux[0:2 * R, BANK + P:BANK + 2 * P]).then_inc(m_hd, 1)
                    act.wait_ge(d_ready, t)
                    act.activation(gate[:, 24:25], gate[:, 25:26], ACT.Exp).then_inc(e_ready, 1)
                if ahead:
                    x_high(t + 1, 1 - h, 1)
                if finish:
                    act.wait_ge(g_tr, t)
                    act.copy(hgt_h[:], aux[:, BANK + 2 * P:BANK + 3 * P]).then_inc(g_hd, 1)
                    act.wait_ge(o_done, t)
                    act.wait_ge(out_done[1 - h], (b + h) * 16)
                    act.copy(out_sb[:, 1 - h, 0:BANK], acc[:, 1 - h, 0:BANK]).then_inc(o_act, 1)

            tile_schedule(act, tile)

        @block.vector
        def _(dve):
            link = Chain(dve, dve_chain)
            dve.wait_ge(bank_in, 64)
            link(dve.tensor_scalar(tmp8[:, 0:LEVELS], book[:], -1.0, None, ALU.mult))
            link(dve.tensor_tensor(tmp8[:, 0:LEVELS], tmp8[:, 0:LEVELS], book[:], ALU.max))
            link(dve.tensor_reduce(tmp8[:, 8:9], tmp8[:, 0:LEVELS], AX.X, ALU.max))
            link(dve.tensor_scalar(tmp8[:, 9:10], tmp8[:, 8:9], 1e-8, None, ALU.max))
            link(dve.reciprocal(tmp8[:, 10:11], tmp8[:, 9:10]))
            link(dve.tensor_scalar(book[:], book[:], tmp8[:, 10:11], None, ALU.mult))
            link(dve.tensor_tensor(thr[:, 0:7], book[:, 0:7], book[:, 1:8], ALU.add))
            link(dve.tensor_scalar(thr[:, 0:7], thr[:, 0:7], 0.5, None, ALU.mult))
            link(dve.tensor_tensor(steps[:, 0:7], book[:, 1:8], book[:, 0:7], ALU.subtract))

            def th(j):
                return thr[:, j:j + 1]
            link(dve.tensor_tensor(th(1), th(1), th(3), ALU.min))
            link(dve.tensor_tensor(th(5), th(5), th(3), ALU.max))
            link(dve.tensor_tensor(th(0), th(0), th(1), ALU.min))
            link(dve.tensor_tensor(th(6), th(6), th(5), ALU.max))
            link(dve.tensor_scalar(th(2), th(2), th(1), th(3), ALU.max, ALU.min))
            link(dve.tensor_scalar(th(4), th(4), th(3), th(5), ALU.max, ALU.min))
            xs, n_f, r_, p_ = scale[:], rscale[:], exp_t[:, 0], exp_t[:, 1]
            link(dve.tensor_scalar(xs, xs, EXP_LOW, EXP_HIGH, ALU.max, ALU.min))
            link(dve.tensor_scalar(n_f, xs, LOG2E, ROUND, ALU.mult, ALU.add))
            link(dve.tensor_scalar(n_f, n_f, ROUND, None, ALU.subtract))
            link(dve.scalar_tensor_tensor(out=r_, in0=n_f, scalar=-LN2_HIGH, in1=xs, op0=ALU.mult, op1=ALU.add))
            link(dve.scalar_tensor_tensor(out=r_, in0=n_f, scalar=-LN2_LOW, in1=r_, op0=ALU.mult, op1=ALU.add))
            link(dve.tensor_scalar(p_, r_, 1.0 / factorial(EXP_TERMS), None, ALU.mult))
            for d in range(EXP_TERMS - 1, 0, -1):
                link(dve.scalar_tensor_tensor(out=p_, in0=p_, scalar=1.0 / factorial(d), in1=r_,
                                              op0=ALU.add, op1=ALU.mult))
            link(dve.tensor_scalar(p_, p_, 1.0, None, ALU.add))
            link(dve.tensor_scalar(n_f, n_f, 127.0, float(1 << 23), ALU.add, ALU.mult))
            link(dve.tensor_copy(exp_n[:], n_f))
            link(dve.tensor_tensor(xs, p_, exp_n[:].bitcast(F32), ALU.mult))
            dve.reciprocal(rscale[:], xs).then_inc(tables, 1)
            dve.wait_ge(small_in, 80)
            nb = 2 * BATCH
            link(dve.tensor_copy(labf[:, 0:nb], labi[:]))
            link(dve.tensor_scalar(labf[:, nb:], labf[:, 0:nb], 0.0, float(LABELS), ALU.is_lt, ALU.mult))
            link(dve.tensor_tensor(labf[:, 0:nb], labf[:, 0:nb], labf[:, nb:], ALU.add))
            link(dve.tensor_scalar(labf[:, 0:nb], labf[:, 0:nb], 0.0, LABELS - 1.0, ALU.max, ALU.min))
            dve.tensor_copy(labu[:], labf[:, 0:nb]).then_inc(tables, 1)
            dve.wait_ge(made, 3)
            link(dve.tensor_copy(iota_f[:], iota_i[:]))
            link(dve.tensor_copy(lab7f[:], lab7i[:]))
            for b in range(BATCH):
                last = dve.tensor_scalar(bias7[:, b, :], iota_f[:], lab7f[:, b:b + 1], 5.0, ALU.is_equal, ALU.mult)
            link(last)
            for n, (raw, hi, lo) in enumerate(((b2raw, b2h, b2l), (b0raw, b0h, b0l))):
                dve.wait_ge(b_hi, n + 1)
                dve.scalar_tensor_tensor(out=lo[:], in0=raw[:], scalar=0.5, in1=hi[:].bitcast(F32),
                                         op0=ALU.mult, op1=ALU.subtract).then_inc(b_split, 1)
            for k in range(KT):
                dve.wait_ge(split_hi, k + 1)
                dve.tensor_tensor(h_lo[:, k, 0:C_LOW2], acc[:, k % 2, 0:C_LOW2], h_hi[:, k, 0:C_LOW2].bitcast(F32),
                                  ALU.subtract).then_inc(h_ready, 1)

            def low(src, h, count):
                dve.wait_ge(w_hi_done, count)
                dve.tensor_tensor(w_lo[:, h], src, w_hi[:, h].bitcast(F32), ALU.subtract).then_inc(w_split, 1)

            low(w_st[:, 0], 0, 1)
            low(w_st[:, 1], 1, 2)

            def quantise(m, h, slot):
                n = w1_st[:, h]
                q = w1_eff[:, slot]
                dve.wait_ge(n_ready, m + 1)
                link(dve.tensor_scalar(q, n, th(0), steps[:, 0:1], ALU.is_gt, ALU.mult))
                for j in range(1, LEVELS - 1):
                    link(dve.tensor_scalar(qtmp[:], n, th(j), steps[:, j:j + 1], ALU.is_gt, ALU.mult))
                    link(dve.tensor_tensor(q, q, qtmp[:], ALU.add))
                dve.scalar_tensor_tensor(out=q, in0=q, scalar=book[:, 0:1],
                                         in1=scale[:, :, bass.ds(m, 1)].to_broadcast([P, KT, P]),
                                         op0=ALU.add, op1=ALU.mult).then_inc(q_ready, 1)

            def step(j, m, h, src, count):
                dve.wait_ge(acc_done, m + (STEP0[j] + 1))
                low(src, h, count)

            def turn(j):
                for k in range(KT):
                    wait_tile_used(dve, j, k)
                    dve.wait_ge(split_hi, KT * (j + 1) + k + 1)
                    dve.tensor_tensor(h_lo[:, k, :], g[:, k, :], h_hi[:, k, :].bitcast(F32),
                                      ALU.subtract).then_inc(h_ready, 1)

            per = 2 * (1 + 2 * (LEVELS - 2))
            at = link.n
            with dve.Fori(0, HALF // 2) as i:
                link.n = i * per + at
                for h in range(2):
                    m = i * 2 + h
                    quantise(m, h, m)
                    step(0, m, h, w_st[:, h], m + 3)
            link.n = at + per * (HALF // 2)
            for m in (4, 5):
                step(0, m, m % 2, w_st[:, m % 2], m + 3)
            for m in (6, 7):
                step(0, m, m % 2, w1_eff[:, m - 6], m + 3)
            turn(0)
            at = link.n
            with dve.Fori(0, HALF // 2) as i:
                link.n = i * per + at
                for h in range(2):
                    m = i * 2 + h
                    dve.wait_ge(w_split, m + (KT + 1))
                    quantise(m + HALF, h, m)
                    step(1, m, h, w1_eff[:, i * (-2) + (2 + h)], m + (KT + 3))
            link.n = at + per * (HALF // 2)
            for m in (4, 5):
                step(1, m, m % 2, w1_eff[:, m - 2], m + KT + 3)
            for m in (6, 7):
                step(1, m, m % 2, w_st[:, m % 2], m + KT + 3)
            turn(1)
            dve.wait_ge(a0_hd, 1)
            dve.tensor_tensor(a0_lo[:], a0_raw[:], a0_hi[:].bitcast(F32), ALU.subtract).then_inc(a0_done, 1)
            with dve.Fori(0, KT // 2 - 1) as i:
                for h in range(2):
                    m = i * 2 + h
                    step(2, m, h, w_st[:, h], m + (2 * KT + 3))
            dve.wait_ge(b3_hd, 1)
            dve.tensor_tensor(b3_lo[:], aux[:, :], b3_hi[:].bitcast(F32), ALU.subtract).then_inc(b3_done, 1)

            def x_low(t, h, half):
                dve.wait_ge(x_hd, t * 2 + (half + 1))
                ks = slice(half * HALF, (half + 1) * HALF)
                dve.tensor_tensor(xt_lo[:, h, ks, :], aux[:, 0:BANK].rearrange("p (k i) -> p k i", k=HALF),
                                  xt_hi[:, h, ks, :].bitcast(F32), ALU.subtract).then_inc(x_split, 1)

            x_low(0, 0, 0)
            turn(2)
            dve.wait_ge(vb_hd, 2)
            dve.tensor_tensor(c_lo[:], bp[0:R, C_LOW2:C_ALL], c_hi[:].bitcast(F32), ALU.subtract).then_inc(vb_done, 1)
            dve.tensor_tensor(vb_lo[:], bp[:, 0:C_LOW2], vb_hi[:].bitcast(F32), ALU.subtract).then_inc(vb_done, 1)
            x_low(0, 0, 1)
            dve.wait_ge(zeroed, 3)

            def tile(t, b, h, finish, ahead):
                s = 1 - h
                if finish:
                    dve.wait_ge(main_done, t)
                    dve.tensor_copy(v_sb[:, 0:2 * R], acc[:, s, V0:V0 + 2 * R]).then_inc(v_out, 1)
                    dve.wait_ge(v_hd, t)
                    dve.tensor_tensor(vt_l[:], aux[0:2 * R, BANK:BANK + P], vt_h[:].bitcast(F32),
                                      ALU.subtract).then_inc(v_split, 1)
                if ahead:
                    x_low(t + 1, s, 0)
                if finish:
                    dve.wait_ge(m_hd, t)
                    dve.tensor_tensor(vm_l[:], aux[0:2 * R, BANK + P:BANK + 2 * P], vm_h[:].bitcast(F32),
                                      ALU.subtract).then_inc(m_split, 1)
                    lg, top, idx, g0, g1 = (gate[:, 8 * n:8 * n + 8] for n in (0, 1, 2, 4, 5))
                    link.n = t * GLINKS + (base - GLINKS)
                    dve.wait_ge(r_done, t)
                    link(dve.tensor_tensor(lg, acc[:, s, C_LOGIT:C_LOW2], bias7[:, b - 1 + h, :], ALU.add))
                    dve.sem_inc(logits_seen, 1)
                    link(dve.max(top, lg))
                    dve.tensor_tensor(gate[:, 25:26], gate[:, 9:10], gate[:, 8:9], ALU.subtract).then_inc(d_ready, 1)
                    link(dve.max_index(top_i[:], top, lg))
                    link(dve.tensor_copy(idx[:, 0:2], top_i[:, 0:2]))
                    dve.wait_ge(e_ready, t)
                    link(dve.tensor_scalar(gate[:, 26:27], gate[:, 24:25], 1.0, 0.5, ALU.add, ALU.mult))
                    link(dve.reciprocal(gate[:, 27:28], gate[:, 26:27]))
                    link(dve.tensor_scalar(gate[:, 28:29], gate[:, 27:28], gate[:, 24:25], None, ALU.mult))
                    link(dve.tensor_scalar(g0, iota_f[:], idx[:, 0:1], gate[:, 27:28], ALU.is_equal, ALU.mult))
                    link(dve.tensor_scalar(g1, iota_f[:], idx[:, 1:2], gate[:, 28:29], ALU.is_equal, ALU.mult))
                    link(dve.tensor_tensor(g0, g0, g1, ALU.add))
                    dve.tensor_tensor(hg[:], acc[:, s, C_H:C_LOGIT].rearrange("p (e r) -> p e r", e=E),
                                      g0.unsqueeze(2).to_broadcast([P, E, RE]), ALU.mult).then_inc(hg_ready, 1)
                if ahead:
                    x_low(t + 1, s, 1)
                if finish:
                    dve.wait_ge(g_hd, t)
                    dve.tensor_tensor(hgt_l[:], aux[:, BANK + 2 * P:BANK + 3 * P], hgt_h[:].bitcast(F32),
                                      ALU.subtract).then_inc(g_split, 1)
                    dve.wait_ge(o_done, t)
                    dve.wait_ge(out_done[s], (b + h) * 16)
                    dve.tensor_copy(out_sb[:, s, BANK:D], acc[:, s, BANK:D]).then_inc(o_dve, 1)

            base = link.n

            tile_schedule(dve, tile)

        @block.tensor
        def _(pe):
            def turn_tile(dst, src, **kw):
                return pe.transpose(dst, src, ident[0:src.shape[0], 0:src.shape[0]])

            pe.wait_ge(made, 2)
            pe.wait_ge(a3_in, 32)
            for k in range(KT):
                pe.wait_ge(w3_eye, k + 1)
                if k >= 2:
                    pe.wait_ge(h_ready, k - 1)
                for n in range(KT):
                    turn_tile(acc[:, k % 2, n * P:(n + 1) * P], g[:, n, k * P:(k + 1) * P])
                turn_tile(acc[:, k % 2, C_H:C_LOGIT], w1_eff[:, 0, k, :])
                turn_tile(acc[:, k % 2, C_LOGIT:C_LOW2], w1_eff[0:E, 1, k, :]).then_inc(w3_t, 1)
            pe.wait_ge(bank_in, 64)
            b1 = w1_eff[:, 2, 0:HALF].rearrange("p k i -> p (k i)").rearrange("p (k r) -> p k r", r=R1)
            for k in range(KT):
                last = turn_tile(aux[0:R1, k * P:(k + 1) * P], b1[:, k, :])
            last.then_inc(b1_t, 1)

            def delta(m):
                pe.wait_ge(aux_free, m + 1)
                for k in range(KT):
                    last = pe.matmul(aux[:, k * P:(k + 1) * P], b1t[:, k * P:(k + 1) * P],
                                     a1[:, bass.ds(m * P, P)], start=True, stop=True)
                last.then_inc(ld_done, 1)

            def one_pass(j, slot, w_h, w_l, rows):
                width = W_IN[j]
                for k in range(KT):
                    pe.wait_ge(h_ready, KT * j + k + 1)
                    for n, (a, b) in enumerate(((w_h, h_hi), (w_h, h_lo), (w_l, h_hi))):
                        for c0, c1 in chunks(width):
                            last = pe.matmul(acc[0:rows, slot, c0:c1], a[:, k, :], b[:, k, c0:c1],
                                             start=(k == 0 and n == 0), stop=(k == KT - 1 and n == 2))
                    last.then_inc(h_used if k < KT - 1 else acc_done, 1)

            def step(j, m, h):
                pe.wait_ge(w_split, m + (KT * j + 1))
                pe.wait_ge(acc_free, m + (STEP0[j] + 1))
                one_pass(j, (STEP0[j] + h) % 2, w_hi[:, h], w_lo[:, h], P)

            pe.wait_ge(h_ready, KT)
            for j in range(2):
                with pe.Fori(0, HALF // 2) as i:
                    for h in range(2):
                        m = i * 2 + h
                        delta(m + j * HALF)
                        step(j, m, h)
                with pe.Fori(HALF // 2, KT // 2) as i:
                    for h in range(2):
                        step(j, i * 2 + h, h)
                if j == 0:
                    pe.wait_ge(b_split, 2)
                    pe.wait_ge(acc_free, KT + 1)
                    one_pass(0, 0, b2h, b2l, R)
            with pe.Fori(0, KT // 2 - 1) as i:
                for h in range(2):
                    step(2, i * 2 + h, h)
            pe.wait_ge(b3_in, 16 * E)
            pe.wait_ge(aux_free, KT + 1)
            for k in range(KT):
                last = turn_tile(aux[:, k * P:(k + 1) * P], b3_raw[:, k].rearrange("p e r -> p (e r)"))
            last.then_inc(b3_t, 1)
            for m in (6, 7):
                step(2, m, m % 2)

            def x_turn(t, h, half, load):
                pe.wait_ge(x_in[h], 16 * load)
                if not isinstance(t, int) or t or half:
                    pe.wait_ge(x_split, t * 2 + half)
                for k in range(HALF):
                    kk = half * HALF + k
                    last = turn_tile(aux[:, k * P:(k + 1) * P], x_st[:, h, kk * P:(kk + 1) * P])
                last.then_inc(x_tr, 1)

            pe.wait_ge(b3_done, 1)
            x_turn(0, 0, 0, 1)
            pe.wait_ge(acc_free, PASSES)
            one_pass(2, 1, b0h, b0l, R)
            x_turn(0, 0, 1, 1)
            pe.wait_ge(h_ready, 4 * KT)

            def three(dst, a, b, start=False, stop=False, **kw):
                (ah, al), (bh, bl) = a, b
                for n, (p, q) in enumerate(((ah, bh), (ah, bl), (al, bh))):
                    last = pe.matmul(dst, p, q, start=start and n == 0, stop=stop and n == 2, skip_group_check=True)
                return last

            def tile(t, b, h, finish, ahead):
                s = 1 - h

                def big(k):
                    for n, (a, b) in enumerate(((xt_hi, h_hi), (xt_hi, h_lo), (xt_lo, h_hi))):
                        for c0, c1 in chunks(D):
                            pe.matmul(acc[:, h, c0:c1], a[:, h, k, :], b[:, k, c0:c1],
                                      start=(k == 0 and n == 0), stop=False, skip_group_check=True)

                def small(k):
                    for n, (a, b, c) in enumerate(((xt_hi, h_hi, sel_hi), (xt_hi, h_lo, sel_lo), (xt_lo, h_hi, sel_hi))):
                        pe.matmul(acc[:, h, C_H:C_LOW2], a[:, h, k, :], b[:, k, C_H:C_LOW2],
                                  start=(k == 0 and n == 0), stop=False, skip_group_check=True)
                        last = pe.matmul(acc[:, h, V0:V0 + 2 * R], a[:, h, k, :], c[:, h, k, :],
                                         start=False, stop=(k == KT - 1 and n == 2), skip_group_check=True)
                    return last

                if ahead is not None:
                    pe.wait_ge(x_split, t * 2 + 2)
                    if finish:
                        if not isinstance(t, int) or t >= 2:
                            pe.wait_ge(o_act, t - 1)
                            pe.wait_ge(o_dve, t - 1)
                            pe.wait_ge(hg_ready, t - 1)
                for k in range(KT):
                    if ahead is not None:
                        big(k)
                        if finish:
                            if k == 0:
                                pe.wait_ge(sel_ready, t * SELS + SELS)
                            last = small(k)
                    if finish and k == 0:
                        pe.wait_ge(v_out, t)
                        turn_tile(aux[:, BANK:BANK + P], v_sb[:]).then_inc(v_tr, 1)
                    if ahead and k == 1:
                        x_turn(t + 1, s, 0, b + 1 + h)
                    if finish and k == 2:
                        pe.wait_ge(v_split, t)
                        three(aux[:, BANK + P:BANK + 2 * P], (tsel_h[:, s], tsel_l[:, s]), (vt_h[:], vt_l[:]),
                              True, True).then_inc(mix_done, 1)
                    if finish and k == 3:
                        pe.wait_ge(m_split, t)
                        three(acc[:, s, C_H:C_LOW2], (vm_h[:], vm_l[:]),
                              (vb_hi[:, C_H:C_LOW2], vb_lo[:, C_H:C_LOW2]), stop=True).then_inc(r_done, 1)
                        for c0, c1 in chunks(D):
                            three(acc[:, s, c0:c1], (vm_h[:], vm_l[:]), (vb_hi[:, c0:c1], vb_lo[:, c0:c1]))
                    if ahead and k == 4:
                        x_turn(t + 1, s, 1, b + 1 + h)
                    if finish and k == 5:
                        pe.wait_ge(hg_ready, t)
                        turn_tile(aux[:, BANK + 2 * P:BANK + 3 * P],
                                  hg[:].rearrange("p e r -> p (e r)")).then_inc(g_tr, 1)
                    if finish and k == 6:
                        pe.wait_ge(g_split, t)
                        for c0, c1 in chunks(D):
                            done = three(acc[:, s, c0:c1], (hgt_h[:], hgt_l[:]), (b3_hi[:, c0:c1], b3_lo[:, c0:c1]),
                                         stop=True)
                        done.then_inc(o_done, 1)
                if ahead is not None:
                    if not finish:
                        pe.wait_ge(sel_ready, SELS)
                        for k in range(KT):
                            last = small(k)
                    last.then_inc(main_done, 1)

            tile_schedule(pe, tile)
    return nc


_INS = ['x', 'itok_B_0_4', 'condB_codebook', 'itok_B_0_2', 'itok_B_0_7', 'L0_cond_weight', 'L0_cond_lora_A',
        'L0_cond_lora_B_w', 'L1_cond_weight', 'L1_cond_scale_log', 'L1_cond_lora_A', 'L1_cond_lora_B',
        'L2_cond_W', 'L2_cond_lora_A', 'L2_cond_lora_B_w', 'L3_cond_W', 'L3_cond_Wr', 'L3_cond_A', 'L3_cond_B']


def kernel(**inputs):
    import numpy as _np
    import concourse.bacc as _bacc
    from concourse import mybir as _mybir
    from concourse.bass_utils import run_bass_kernel_spmd as _run

    nc = _bacc.Bacc("TRN2", target_bir_lowering=False, num_devices=1)
    arrays, args = {}, []
    for name in _INS:
        a = _np.ascontiguousarray(inputs[name])
        arrays[f"in_{name}_dram"] = a
        args.append(nc.dram_tensor(f"in_{name}_dram", a.shape, _mybir.dt.from_np(a.dtype), kind="ExternalInput").ap())
    shape = inputs['x'].shape
    args.append(nc.dram_tensor("out_0_dram", shape, _mybir.dt.float32, kind="ExternalOutput").ap())
    build(nc, *args)
    r = _run(nc, [arrays], core_ids=[0])
    return r.results[0]["out_0_dram"]
```

```python
from contextlib import ExitStack
from math import factorial

import concourse.bass as bass
from concourse import mybir

ALU = mybir.AluOpType
ACT = mybir.ActivationFunctionType
AX = mybir.AxisListType
F32 = mybir.dt.float32
F32R = mybir.dt.float32r
I32 = mybir.dt.int32
U32 = mybir.dt.uint32

P = 128
LOG2E = 1.4426950408889634
LN2_HIGH = 0.693359375
LN2_LOW = -2.12194440054690583e-4
ROUND = 1.5 * (1 << 23)
EXP_TERMS = 8
EXP_LOW, EXP_HIGH = -87.0, 88.0
BANK = 512


class Chain:

    def __init__(self, eng, sem):
        self.eng, self.sem, self.n = eng, sem, 0

    def __call__(self, instruction):
        instruction.then_inc(self.sem, 1)
        self.n = self.n + 1
        self.eng.wait_ge(self.sem, self.n)


def build(nc, x, lab0, codebook, lab2, lab7, W0, A0, B0, W1, scale_log, A1, B1, W2, A2, B2, W3, Wr, A3, B3, out):
    BATCH, SEQ, D = x.shape
    LABELS, _, R = A0.shape
    R1 = A1.shape[0]
    E, RE, _ = A3.shape
    ER = E * RE
    KT = D // P
    G1 = scale_log.shape[1]
    LEVELS = codebook.shape[0]
    TILES = BATCH * SEQ // P
    PER_BATCH = SEQ // P
    C_H, C_LOGIT, C_LOW2 = D, D + ER, D + ER + E
    C_ALL = C_LOW2 + LABELS * R
    NR = ER + E
    assert (D, PER_BATCH, D // G1, ER, KT, LEVELS, R1, R) == (1024, 2, P, P, 8, 8, 64, 32)
    W_IN = (C_LOW2, C_ALL, C_ALL)
    STEP0 = (0, KT + 1, 2 * KT + 1)
    PASSES = 3 * KT + 2
    HALF = KT // 2
    SLOTS = 4
    QUANT = ({1: 0, 2: 1, 4: 2, 6: 3}, {0: 4, 1: 5, 3: 6, 5: 7})

    def chunks(width):
        return [(c, min(width, c + BANK)) for c in range(0, width, BANK)]

    def thirds(width):
        part = -(-width // 6) * 2
        return [(n * part, min(width, (n + 1) * part)) for n in range(3)]

    with ExitStack() as ctx:
        def sb(name, shape, dt=F32, stack=ctx):
            return stack.enter_context(nc.sbuf_tensor(name, shape, dt))

        def sem(name):
            return ctx.enter_context(nc.semaphore(name))

        h_hi = sb("h_hi", [P, KT, C_ALL], F32R)
        h_lo = sb("h_lo", [P, KT, C_ALL], F32R)
        ident = sb("ident", [P, P])
        bp = sb("bp", [2 * R, C_ALL])
        b2raw, b0raw = sb("b2raw", [P, KT, R]), sb("b0raw", [P, KT, R])
        b2h, b2l = sb("b2h", [P, KT, R], F32R), sb("b2l", [P, KT, R], F32R)
        b0h, b0l = sb("b0h", [P, KT, R], F32R), sb("b0l", [P, KT, R], F32R)
        scale, rscale = sb("scale", [P, KT, G1]), sb("rscale", [P, KT, G1])
        exp_t, exp_n = sb("exp_t", [P, 2, KT, G1]), sb("exp_n", [P, KT, G1], I32)
        book = sb("book", [P, LEVELS])
        steps = sb("steps", [P, LEVELS])
        thr = sb("thr", [P, LEVELS])
        tmp8 = sb("tmp8", [P, 2 * LEVELS])
        labi = sb("labi", [1, 2 * BATCH], I32)
        labf = sb("labf", [1, 4 * BATCH])
        labu = sb("labu", [1, 2 * BATCH], I32)
        lab7i = sb("lab7i", [P, BATCH], I32)
        lab7f = sb("lab7f", [P, BATCH])
        iota_i = sb("iota_i", [P, E], I32)
        iota_f = sb("iota_f", [P, E])
        bias7 = sb("bias7", [P, BATCH, E])

        first = ExitStack()
        g = sb("g", [P, KT, C_ALL], F32, first)
        w1_st = sb("w1_st", [P, 2, KT, P], F32, first)
        w1_eff = sb("w1_eff", [P, SLOTS, KT, P], F32, first)
        ldelta = sb("ldelta", [P, KT, P], F32, first)
        qtmp = sb("qtmp", [P, KT, P], F32, first)
        a1 = sb("a1", [R1, D], F32, first)
        b1t = sb("b1t", [R1, D], F32, first)
        w_hi = sb("w_hi", [P, 2, KT, P], F32R, first)
        w_lo = sb("w_lo", [P, 2, KT, P], F32R, first)
        w_st = sb("w_st", [P, 2, KT, P], F32, first)
        first.close()
        second = ctx
        vb_hi, vb_lo = sb("vb_hi", [2 * R, C_LOW2], F32R), sb("vb_lo", [2 * R, C_LOW2], F32R)
        c_hi, c_lo = sb("c_hi", [R, LABELS * R], F32R), sb("c_lo", [R, LABELS * R], F32R)
        tsel_h, tsel_l = sb("tsel_h", [2 * R, 2, P], F32R), sb("tsel_l", [2 * R, 2, P], F32R)
        out_sb = sb("out_sb", [P, 2, D])
        v_sb = sb("v_sb", [P, P])
        vt_h, vt_l = sb("vt_h", [2 * R, P], F32R), sb("vt_l", [2 * R, P], F32R)
        vm_h, vm_l = sb("vm_h", [2 * R, P], F32R), sb("vm_l", [2 * R, P], F32R)
        hg = sb("hg", [P, E, RE])
        hgt_h, hgt_l = sb("hgt_h", [P, P], F32R), sb("hgt_l", [P, P], F32R)
        gate = sb("gate", [P, 96])
        top_i = sb("top_i", [P, 8], U32)
        sel_hi = sb("sel_hi", [P, 2, KT, NR + 2 * R], F32R)
        used = 2 * KT * (NR + 2 * R) + 2 * C_LOW2 + 2 * LABELS * R + 4 * P + 2 * D + P + 4 * P + P + 2 * P + 96 + 8
        sb("pad", [P, KT * C_ALL - used])
        a0_raw = sb("a0_raw", [P, KT, LABELS * R])
        a0_hi, a0_lo = sb("a0_hi", [P, KT, LABELS * R], F32R), sb("a0_lo", [P, KT, LABELS * R], F32R)
        b3_raw = sb("b3_raw", [P, KT, E, RE])
        b3_hi, b3_lo = sb("b3_hi", [P, D], F32R), sb("b3_lo", [P, D], F32R)
        sel_lo = sb("sel_lo", [P, 2, KT, NR + 2 * R], F32R)
        sb("pad2", [P, (6 + SLOTS) * D - 3 * KT * LABELS * R - 3 * D - 2 * KT * (NR + 2 * R)])
        xt_hi, xt_lo = sb("xt_hi", [P, 2, KT, P], F32R), sb("xt_lo", [P, 2, KT, P], F32R)
        x_st = sb("x_st", [P, 2, D])

        acc = ctx.enter_context(nc.psum_tensor("acc", [P, 2, 3 * BANK], F32))
        aux = ctx.enter_context(nc.psum_tensor("aux", [P, 2 * BANK], F32))
        V0 = D + NR

        w3_in = [sem(f"w3_in{k}") for k in range(KT)]
        small_in, bank_in, a3_in, a2_in = sem("small_in"), sem("book_in"), sem("a3_in"), sem("a2_in")
        w_in = [sem(f"w_in{i}") for i in range(2)]
        w1_in = sem("w1_in")
        a0_in, b3_in = sem("a0_in"), sem("b3_in")
        x_in = [sem(f"x_in{i}") for i in range(2)]
        out_done = [sem(f"out_done{i}") for i in range(2)]
        made = sem("made")
        w3_eye = sem("w3_eye")
        w3_t = sem("w3_t")
        split_hi = sem("split_hi")
        h_ready = sem("h_ready")
        h_used = sem("h_used")
        acc_done = sem("acc_done")
        acc_free = sem("acc_free")
        acc_part = sem("acc_part")
        w_eye = sem("w_eye")
        w_hi_done = sem("w_hi_done")
        w_split = sem("w_split")
        b_hi, b_split = sem("b_hi"), sem("b_split")
        b1_t = sem("b1_t")
        tables = sem("tables")
        ld_done, aux_free = sem("ld_done"), sem("aux_free")
        v_ready = sem("v_ready")
        q_ready, q_sum, w1e_done = sem("q_ready"), sem("q_sum"), sem("w1e_done")
        dve_chain = sem("dve_chain")
        a0_hd, a0_done = sem("a0_hd"), sem("a0_done")
        b3_t, b3_hd, b3_done = sem("b3_t"), sem("b3_hd"), sem("b3_done")
        vb_hd, vb_done = sem("vb_hd"), sem("vb_done")
        zeroed, eyed = sem("zeroed"), sem("eyed")
        x_tr, x_hd, x_split = sem("x_tr"), sem("x_hd"), sem("x_split")
        sel_fixed, sel_ready, tsel_ready = sem("sel_fixed"), sem("sel_ready"), sem("tsel_ready")
        main_done = sem("main_done")
        v_out, v_tr, v_hd, v_split = sem("v_out"), sem("v_tr"), sem("v_hd"), sem("v_split")
        mix_done, m_hd, m_split = sem("mix_done"), sem("m_hd"), sem("m_split")
        logits_seen = sem("logits_seen")
        r_done, d_ready, e_ready = sem("r_done"), sem("d_ready"), sem("e_ready")
        hg_ready, g_tr, g_hd, g_split = sem("hg_ready"), sem("g_tr"), sem("g_hd"), sem("g_split")
        o_done, o_act, o_dve = sem("o_done"), sem("o_act"), sem("o_dve")

        GLINKS = 10
        SELS = 4

        x_rows = x.rearrange("b s d -> (b s) d")
        out_rows = out.rearrange("b s d -> (b s) d")

        def slices(w):
            return w.rearrange("(k p) i -> p k i", p=P)

        def wait_tile_used(eng, j, k):
            last = STEP0[j] + KT - 1 + (j != 1)
            if k < KT - 1:
                eng.wait_ge(h_used, (KT - 1) * last + k + 1)
            else:
                eng.wait_ge(acc_done, last + 1)

        def tile_schedule(eng, tile):
            tile(0, 0, 0, False, True)
            tile(1, 0, 1, True, True)
            with eng.Fori(1, BATCH - 1) as b:
                for h in range(2):
                    tile(b * 2 + h, b, h, True, True)
            tile(TILES - 2, BATCH - 1, 0, True, True)
            tile(TILES - 1, BATCH - 1, 1, True, False)
            tile(TILES, BATCH, 0, True, None)

        block = ctx.enter_context(nc.Block())

        @block.sync
        def _(sp):
            for h in range(2):
                sp.sem_inc(out_done[h], 16)
            for k in range(KT):
                sp.dma_start(g[:, :, k * P:(k + 1) * P], slices(W3)[:, :, k * P:(k + 1) * P]).then_inc(w3_in[k], 16)
                if k == 0:
                    sp.dma_start(w1_eff[:, 0].rearrange("p k i -> p (k i)"),
                                 A3.rearrange("e r d -> (e r) d")).then_inc(a3_in, 16)
                    sp.dma_start(w1_eff[0:E, 1].rearrange("p k i -> p (k i)"), Wr).then_inc(a3_in, 16)
            for u in range(2):
                sp.dma_start(w_st[:, u], slices(W2)[:, :, u * P:(u + 1) * P]).then_inc(w_in[u], 16)
            sp.dma_start(book[:], codebook.rearrange("(a c) -> a c", a=1).to_broadcast([P, LEVELS])).then_inc(bank_in, 16)
            sp.dma_start(scale[:], scale_log.rearrange("(k p) g a -> p k (g a)", p=P)).then_inc(bank_in, 16)
            sp.dma_start(w1_eff[:, 2, 0:HALF].rearrange("p k i -> p (k i)").rearrange("p (k r) -> p k r", r=R1),
                         B1.rearrange("(k p) r -> p k r", p=P)).then_inc(bank_in, 16)
            sp.dma_start(a1[:], A1).then_inc(bank_in, 16)
            sp.dma_start(w1_st[:, 0], slices(W1)[:, :, 0:P]).then_inc(w1_in, 16)
            sp.dma_start(labi[0:1, 0:BATCH], lab0.rearrange("(a c) -> a c", a=1)).then_inc(small_in, 16)
            sp.dma_start(labi[0:1, BATCH:], lab2.rearrange("(a c) -> a c", a=1)).then_inc(small_in, 16)
            sp.dma_start(lab7i[:], lab7.rearrange("(a c) -> a c", a=1).to_broadcast([P, BATCH])).then_inc(small_in, 16)
            sp.dma_start(b2raw[:], B2.rearrange("(k p) r -> p k r", p=P)).then_inc(small_in, 16)
            sp.dma_start(b0raw[:], B0.rearrange("(k p) r -> p k r", p=P)).then_inc(small_in, 16)
            for l in range(LABELS):
                sp.dma_start(g[:, :, C_LOW2 + l * R:C_LOW2 + (l + 1) * R],
                             A2[l].rearrange("(k p) r -> p k r", p=P)).then_inc(a2_in, 16)

            def load_w(W, h, cols, need):
                sp.wait_ge(w_split, need)
                sp.dma_start(w_st[:, h], slices(W)[:, :, cols]).then_inc(w_in[h], 16)

            def load_w1(n, h):
                sp.wait_ge(q_ready, n - 1)
                sp.wait_ge(w1_in, n * 16)
                sp.dma_start(w1_st[:, h], slices(W1)[:, :, bass.ds(n * P, P)]).then_inc(w1_in, 16)

            sp.wait_ge(w1_in, 16)
            sp.dma_start(w1_st[:, 1], slices(W1)[:, :, P:2 * P]).then_inc(w1_in, 16)
            for h in range(2):
                load_w(W2, h, bass.ds((2 + h) * P, P), h + 1)
            for m in range(KT - 2):
                if (n := QUANT[0].get(m)) is not None:
                    load_w1(n + 2, n % 2)
                load_w(W2 if m < KT - 4 else W0, m % 2, bass.ds((m + 4) % KT * P, P), m + 3)
            load_w1(5, 1)
            for n in range(6, KT):
                load_w1(n, n % 2)
            sp.wait_ge(w_split, 2 * KT)
            for l in range(LABELS):
                sp.dma_start(a0_raw[:, :, l * R:(l + 1) * R], A0[l].rearrange("(k p) r -> p k r", p=P)).then_inc(a0_in, 16)
            with sp.Fori(0, KT // 2 - 1) as i:
                for h in range(2):
                    m = i * 2 + h
                    load_w(W0, h, bass.ds(m * P + 2 * P, P), m + 2 * KT + 1)
            for e in range(E):
                sp.dma_start(b3_raw[:, :, e], B3[e].rearrange("(k p) r -> p k r", p=P)).then_inc(b3_in, 16)

            sp.wait_ge(w_split, 3 * KT)
            for t in range(2):
                sp.dma_start(x_st[:, t], x_rows[t * P:(t + 1) * P, :]).then_inc(x_in[t], 16)

            def tile_io(t, h, load, store):
                if load:
                    sp.wait_ge(x_tr, t * 2 + 2)
                    sp.dma_start(x_st[:, h], x_rows[bass.ds(t * P + 2 * P, P), :]).then_inc(x_in[h], 16)
                if store:
                    sp.wait_ge(o_act, t + 1)
                    sp.wait_ge(o_dve, t + 1)
                    sp.dma_start(out_rows[bass.ds(t * P, P), :], out_sb[:, h]).then_inc(out_done[h], 16)

            tile_io(0, 0, True, False)
            tile_io(1, 1, True, False)
            with sp.Fori(0, TILES // 2 - 2) as i:
                for h in range(2):
                    t = i * 2 + h
                    tile_io(t + 2, h, True, False)
                    tile_io(t, h, False, True)
            for t in range(TILES - 4, TILES):
                tile_io(t, t % 2, False, True)
            for h in range(2):
                sp.wait_ge(out_done[h], 16 * (TILES // 2 + 1))

        @block.gpsimd
        def _(pool):
            def add_eye(tile, m):
                return pool.tensor_tensor(tile[:, m, :], tile[:, m, :], ident[:], ALU.add)

            pool.sem_inc(q_sum, 1)
            pool.memset(ident[:], 0.0).then_inc(made, 1)
            pool.wait_ge(made, 1)
            pool.affine_select(out=ident[:], in_=ident[:], compare_op=ALU.not_equal, fill=1.0, base=0,
                               pattern=[[-1, P]], channel_multiplier=1).then_inc(made, 1)
            pool.iota(iota_i[:], pattern=[[1, E]], base=0, channel_multiplier=0).then_inc(made, 1)
            pool.wait_ge(made, 3)
            for k in range(KT):
                pool.wait_ge(w3_in[k], 16)
                add_eye(g[:, :, k * P:(k + 1) * P], k).then_inc(w3_eye, 1)

            def eye_w(h, m, load):
                pool.wait_ge(w_in[h], 16 * load)
                add_eye(w_st[:, h], m).then_inc(w_eye, 1)

            def quant_out(m, slot):
                pool.wait_ge(q_ready, m + 1)
                pool.wait_ge(aux_free, m + 2)
                pool.tensor_tensor(w1_eff[:, slot], w1_eff[:, slot], ldelta[:], ALU.add).then_inc(q_sum, 1)
                pool.wait_ge(q_sum, m + 2)
                add_eye(w1_eff[:, slot], m).then_inc(w1e_done, 1)

            for h in range(2):
                eye_w(h, h, 1)
            for m in range(KT):
                n = QUANT[0].get(m)
                eye_w(m % 2, (m + 2) % KT, m // 2 + 2)
                if n is not None:
                    quant_out(n, n % SLOTS)
            for n in QUANT[1].values():
                quant_out(n, n % SLOTS)
            for m in range(2, KT):
                eye_w(m % 2, m, KT // 2 + m // 2 + 1)

            pool.wait_ge(h_ready, 4 * KT)
            pool.wait_ge(a0_done, 1)

            def select(t, b, h, first_use):
                l0 = pool.value_load(labu[0:1, bass.ds(b, 1)], min_val=0, max_val=LABELS - 1)
                l2 = pool.value_load(labu[0:1, bass.ds(b + BATCH, 1)], min_val=0, max_val=LABELS - 1)
                if not first_use:
                    pool.wait_ge(main_done, t - 1)
                for dst, src in ((sel_hi[:, h, :, NR:NR + R], a0_hi[:, :, bass.ds(l0 * R, R)]),
                                 (sel_lo[:, h, :, NR:NR + R], a0_lo[:, :, bass.ds(l0 * R, R)]),
                                 (sel_hi[:, h, :, NR + R:], h_hi[:, :, bass.ds(l2 * R + C_LOW2, R)]),
                                 (sel_lo[:, h, :, NR + R:], h_lo[:, :, bass.ds(l2 * R + C_LOW2, R)])):
                    pool.tensor_copy(dst, src).then_inc(sel_ready, 1)
                if first_use:
                    for n, ts in enumerate((tsel_h, tsel_l)):
                        pool.memset(ts[:, h].bitcast(F32), 0.0).then_inc(zeroed, 1)
                        pool.wait_ge(zeroed, 2 * h + n + 1)
                    pool.tensor_copy(tsel_h[:, h, 0:2 * R], ident[0:2 * R, 0:2 * R]).then_inc(eyed, 1)
                    pool.wait_ge(eyed, h + 1)
                    pool.wait_ge(vb_done, 1)
                else:
                    pool.wait_ge(mix_done, t - 1)
                pool.tensor_copy(tsel_h[0:R, h, R:2 * R], c_hi[:, bass.ds(l2 * R, R)]).then_inc(tsel_ready, 1)
                pool.tensor_copy(tsel_l[0:R, h, R:2 * R], c_lo[:, bass.ds(l2 * R, R)]).then_inc(tsel_ready, 1)

            for h in range(2):
                select(h, 0, h, True)
            with pool.Fori(1, BATCH) as b:
                for h in range(2):
                    select(b * 2 + h, b, h, False)

        @block.scalar
        def _(act):
            act.sem_inc(acc_free, 2)
            for k in range(KT):
                act.wait_ge(w3_t, k + 1)
                act.copy(h_hi[:, k, 0:C_LOW2], acc[:, k % 2, 0:C_LOW2]).then_inc(split_hi, 1)
            act.wait_ge(b1_t, 1)
            act.mul(b1t[:], aux[0:R1, :], 0.5).then_inc(aux_free, 1)

            def high(src, s, h, ready, count):
                act.wait_ge(ready, count)
                act.copy(w_hi[:, h], src).then_inc(w_hi_done, 1)

            def copy_delta(m):
                act.wait_ge(ld_done, m + 1)
                act.wait_ge(v_ready, m + 1)
                act.wait_ge(q_sum, m + 1)
                act.copy(ldelta[:], aux[:, :].rearrange("p (k i) -> p k i", k=KT)).then_inc(aux_free, 1)

            def evacuate(dst, slot, rows, width):
                parts = thirds(width)
                part = parts[0][1]
                banks = acc[0:rows, slot, :].rearrange("p (n c) -> p n c", n=3)
                even = 3 if width == 3 * part else 2
                last = act.copy(dst[:, 0:even * part].rearrange("p (n c) -> p n c", n=even), banks[:, 0:even, 0:part])
                if even == 2:
                    last.then_inc(acc_part, 1)
                    last = act.copy(dst[:, 2 * part:width], banks[:, 2, 0:width - 2 * part])
                last.then_inc(acc_free, 1)

            def turn(j, k0=0, k1=KT):
                act.wait_ge(acc_free, 2 + STEP0[j] + min(k1, KT))
                if j == 0:
                    act.wait_ge(acc_part, KT)
                    act.wait_ge(a2_in, 16 * LABELS)
                for k in range(k0, k1):
                    wait_tile_used(act, j, k)
                    act.copy(h_hi[:, k, :], g[:, k, :]).then_inc(split_hi, 1)

            high(w_st[:, 0], 0, 0, w_eye, 1)
            high(w_st[:, 1], 1, 1, w_eye, 2)
            act.wait_ge(small_in, 80)
            act.mul(b2h[:], b2raw[:], 0.5).then_inc(b_hi, 1)
            act.mul(b0h[:], b0raw[:], 0.5).then_inc(b_hi, 1)

            def step(j, m, h, src, ready, count, delta=None):
                if delta is not None:
                    copy_delta(delta)
                act.wait_ge(acc_done, m + (STEP0[j] + 1))
                if src is not None:
                    high(src, None, h, ready, count)
                evacuate(g[:, m, :], (STEP0[j] + h) % 2, P, W_IN[j])

            for m in range(KT):
                src, ready, count = (w_st[:, m % 2], w_eye, m + 3) if m < KT - 2 else (w1_eff[:, m - 6], w1e_done, m - 5)
                step(0, m, m % 2, src, ready, count, delta=QUANT[0].get(m))
            turn(0)
            act.wait_ge(acc_done, KT + 1)
            evacuate(bp[R:2 * R, :], 0, R, C_LOW2)
            for m in range(KT - 2):
                step(1, m, m % 2, w1_eff[:, (m + 2) % SLOTS], w1e_done, m + 3, delta=QUANT[1].get(m))
            step(1, 6, 0, w_st[:, 0], w_eye, KT + 1)
            turn(1, 0, KT - 1)
            step(1, 7, 1, w_st[:, 1], w_eye, KT + 2)
            turn(1, KT - 1, KT)
            act.wait_ge(a0_in, 16 * LABELS)
            act.copy(a0_hi[:], a0_raw[:]).then_inc(a0_hd, 1)
            with act.Fori(0, KT // 2 - 1) as i:
                for h in range(2):
                    m = i * 2 + h
                    step(2, m, h, w_st[:, h], w_eye, m + (KT + 3))
            act.wait_ge(b3_t, 1)
            act.copy(b3_hi[:], aux[:, :]).then_inc(b3_hd, 1)
            for m in (6, 7):
                step(2, m, m % 2, None, None, None)

            def x_high(t, h, half, c0=0):
                act.wait_ge(x_tr, t * 2 + (half + 1))
                act.copy(xt_hi[:, h, half * HALF:(half + 1) * HALF, :],
                         aux[:, c0:c0 + BANK].rearrange("p (k i) -> p k i", k=HALF)).then_inc(x_hd, 1)

            x_high(0, 0, 0)
            x_high(0, 0, 1, BANK)
            turn(2)
            act.wait_ge(h_ready, 4 * KT)
            for h in range(2):
                act.copy(sel_hi[:, h, :, 0:NR], h_hi[:, :, C_H:C_LOW2]).then_inc(sel_fixed, 1)
            act.wait_ge(acc_done, PASSES)
            evacuate(bp[0:R, :], 1, R, C_ALL)
            act.wait_ge(acc_free, 2 + PASSES)
            act.wait_ge(acc_part, KT + 1)
            act.copy(c_hi[:], bp[0:R, C_LOW2:C_ALL]).then_inc(vb_hd, 1)
            act.copy(vb_hi[:], bp[:, 0:C_LOW2]).then_inc(vb_hd, 1)

            def tile(t, b, h, finish, ahead):
                if finish:
                    act.wait_ge(v_tr, t)
                    act.copy(vt_h[:], aux[0:2 * R, BANK:BANK + P]).then_inc(v_hd, 1)
                if ahead:
                    if finish:
                        act.wait_ge(main_done, t)
                    x_high(t + 1, 1 - h, 0)
                if finish:
                    act.wait_ge(mix_done, t)
                    act.copy(vm_h[:], aux[0:2 * R, BANK + P:BANK + 2 * P]).then_inc(m_hd, 1)
                    act.wait_ge(d_ready, t)
                    act.activation(gate[:, 24:25], gate[:, 25:26], ACT.Exp).then_inc(e_ready, 1)
                if ahead:
                    x_high(t + 1, 1 - h, 1)
                if finish:
                    act.wait_ge(g_tr, t)
                    act.copy(hgt_h[:], aux[:, BANK + 2 * P:BANK + 3 * P]).then_inc(g_hd, 1)
                    act.wait_ge(o_done, t)
                    act.wait_ge(out_done[1 - h], (b + h) * 16)
                    act.copy(out_sb[:, 1 - h, 0:BANK], acc[:, 1 - h, 0:BANK]).then_inc(o_act, 1)

            tile_schedule(act, tile)

        @block.vector
        def _(dve):
            link = Chain(dve, dve_chain)
            for k in range(KT):
                dve.wait_ge(split_hi, k + 1)
                dve.tensor_tensor(h_lo[:, k, 0:C_LOW2], acc[:, k % 2, 0:C_LOW2], h_hi[:, k, 0:C_LOW2].bitcast(F32),
                                  ALU.subtract).then_inc(h_ready, 1)

            def low(src, h, count):
                dve.wait_ge(w_hi_done, count)
                dve.tensor_tensor(w_lo[:, h], src, w_hi[:, h].bitcast(F32), ALU.subtract).then_inc(w_split, 1)

            low(w_st[:, 0], 0, 1)
            low(w_st[:, 1], 1, 2)
            dve.wait_ge(bank_in, 64)
            link(dve.tensor_scalar(tmp8[:, 0:LEVELS], book[:], -1.0, None, ALU.mult))
            link(dve.tensor_tensor(tmp8[:, 0:LEVELS], tmp8[:, 0:LEVELS], book[:], ALU.max))
            link(dve.tensor_reduce(tmp8[:, 8:9], tmp8[:, 0:LEVELS], AX.X, ALU.max))
            link(dve.tensor_scalar(tmp8[:, 9:10], tmp8[:, 8:9], 1e-8, None, ALU.max))
            link(dve.reciprocal(tmp8[:, 10:11], tmp8[:, 9:10]))
            link(dve.tensor_scalar(book[:], book[:], tmp8[:, 10:11], None, ALU.mult))
            link(dve.tensor_tensor(thr[:, 0:7], book[:, 0:7], book[:, 1:8], ALU.add))
            link(dve.tensor_scalar(thr[:, 0:7], thr[:, 0:7], 0.5, None, ALU.mult))
            link(dve.tensor_tensor(steps[:, 0:7], book[:, 1:8], book[:, 0:7], ALU.subtract))

            def th(j):
                return thr[:, j:j + 1]
            link(dve.tensor_tensor(th(1), th(1), th(3), ALU.min))
            link(dve.tensor_tensor(th(5), th(5), th(3), ALU.max))
            link(dve.tensor_tensor(th(0), th(0), th(1), ALU.min))
            link(dve.tensor_tensor(th(6), th(6), th(5), ALU.max))
            link(dve.tensor_scalar(th(2), th(2), th(1), th(3), ALU.max, ALU.min))
            link(dve.tensor_scalar(th(4), th(4), th(3), th(5), ALU.max, ALU.min))
            xs, n_f, r_, p_ = scale[:], rscale[:], exp_t[:, 0], exp_t[:, 1]
            link(dve.tensor_scalar(xs, xs, EXP_LOW, EXP_HIGH, ALU.max, ALU.min))
            link(dve.tensor_scalar(n_f, xs, LOG2E, ROUND, ALU.mult, ALU.add))
            link(dve.tensor_scalar(n_f, n_f, ROUND, None, ALU.subtract))
            link(dve.scalar_tensor_tensor(out=r_, in0=n_f, scalar=-LN2_HIGH, in1=xs, op0=ALU.mult, op1=ALU.add))
            link(dve.scalar_tensor_tensor(out=r_, in0=n_f, scalar=-LN2_LOW, in1=r_, op0=ALU.mult, op1=ALU.add))
            link(dve.tensor_scalar(p_, r_, 1.0 / factorial(EXP_TERMS), None, ALU.mult))
            for d in range(EXP_TERMS - 1, 0, -1):
                link(dve.scalar_tensor_tensor(out=p_, in0=p_, scalar=1.0 / factorial(d), in1=r_,
                                              op0=ALU.add, op1=ALU.mult))
            link(dve.tensor_scalar(p_, p_, 1.0, None, ALU.add))
            link(dve.tensor_scalar(n_f, n_f, 127.0, float(1 << 23), ALU.add, ALU.mult))
            link(dve.tensor_copy(exp_n[:], n_f))
            link(dve.tensor_tensor(xs, p_, exp_n[:].bitcast(F32), ALU.mult))
            dve.reciprocal(rscale[:], xs).then_inc(tables, 1)
            dve.wait_ge(small_in, 80)
            nb = 2 * BATCH
            link(dve.tensor_copy(labf[:, 0:nb], labi[:]))
            link(dve.tensor_scalar(labf[:, nb:], labf[:, 0:nb], 0.0, float(LABELS), ALU.is_lt, ALU.mult))
            link(dve.tensor_tensor(labf[:, 0:nb], labf[:, 0:nb], labf[:, nb:], ALU.add))
            link(dve.tensor_scalar(labf[:, 0:nb], labf[:, 0:nb], 0.0, LABELS - 1.0, ALU.max, ALU.min))
            dve.tensor_copy(labu[:], labf[:, 0:nb]).then_inc(tables, 1)
            dve.wait_ge(made, 3)
            link(dve.tensor_copy(iota_f[:], iota_i[:]))
            link(dve.tensor_copy(lab7f[:], lab7i[:]))
            for b in range(BATCH):
                last = dve.tensor_scalar(bias7[:, b, :], iota_f[:], lab7f[:, b:b + 1], 5.0, ALU.is_equal, ALU.mult)
            link(last)
            for n, (raw, hi, lo) in enumerate(((b2raw, b2h, b2l), (b0raw, b0h, b0l))):
                dve.wait_ge(b_hi, n + 1)
                dve.scalar_tensor_tensor(out=lo[:], in0=raw[:], scalar=0.5, in1=hi[:].bitcast(F32),
                                         op0=ALU.mult, op1=ALU.subtract).then_inc(b_split, 1)

            def quantise(m, h, slot):
                n = w1_st[:, h]
                q = w1_eff[:, slot]
                dve.wait_ge(w1_in, 16 * (m + 1))
                dve.wait_ge(ld_done, m + 1)
                dve.tensor_tensor(n, n, aux[:, :].rearrange("p (k i) -> p k i", k=KT), ALU.add).then_inc(v_ready, 1)
                dve.wait_ge(v_ready, m + 1)
                link(dve.tensor_tensor(n, n, rscale[:, :, m:m + 1].to_broadcast([P, KT, P]), ALU.mult))
                link(dve.tensor_scalar(q, n, th(0), steps[:, 0:1], ALU.is_gt, ALU.mult))
                for j in range(1, LEVELS - 1):
                    link(dve.tensor_scalar(qtmp[:], n, th(j), steps[:, j:j + 1], ALU.is_gt, ALU.mult))
                    link(dve.tensor_tensor(q, q, qtmp[:], ALU.add))
                dve.scalar_tensor_tensor(out=q, in0=q, scalar=book[:, 0:1],
                                         in1=scale[:, :, bass.ds(m, 1)].to_broadcast([P, KT, P]),
                                         op0=ALU.add, op1=ALU.mult).then_inc(q_ready, 1)

            def step(j, m, h, src, count):
                dve.wait_ge(acc_done, m + (STEP0[j] + 1))
                low(src, h, count)

            def turn(j, k0=0, k1=KT):
                for k in range(k0, k1):
                    wait_tile_used(dve, j, k)
                    dve.wait_ge(split_hi, KT * (j + 1) + k + 1)
                    dve.tensor_tensor(h_lo[:, k, :], g[:, k, :], h_hi[:, k, :].bitcast(F32),
                                      ALU.subtract).then_inc(h_ready, 1)

            for m in range(KT):
                if (n := QUANT[0].get(m)) is not None:
                    quantise(n, n % 2, n % SLOTS)
                step(0, m, m % 2, w_st[:, m % 2] if m < KT - 2 else w1_eff[:, m - 6], m + 3)
            turn(0)
            for m in range(KT - 2):
                if (n := QUANT[1].get(m)) is not None:
                    dve.wait_ge(w_split, KT + n - SLOTS + 1)
                    quantise(n, n % 2, n % SLOTS)
                step(1, m, m % 2, w1_eff[:, (m + 2) % SLOTS], m + KT + 3)
            step(1, 6, 0, w_st[:, 0], 2 * KT + 1)
            turn(1, 0, KT - 1)
            step(1, 7, 1, w_st[:, 1], 2 * KT + 2)
            turn(1, KT - 1, KT)
            dve.wait_ge(a0_hd, 1)
            dve.tensor_tensor(a0_lo[:], a0_raw[:], a0_hi[:].bitcast(F32), ALU.subtract).then_inc(a0_done, 1)
            with dve.Fori(0, KT // 2 - 1) as i:
                for h in range(2):
                    m = i * 2 + h
                    step(2, m, h, w_st[:, h], m + (2 * KT + 3))
            dve.wait_ge(b3_hd, 1)
            dve.tensor_tensor(b3_lo[:], aux[:, :], b3_hi[:].bitcast(F32), ALU.subtract).then_inc(b3_done, 1)

            def x_low(t, h, half, c0=0):
                dve.wait_ge(x_hd, t * 2 + (half + 1))
                ks = slice(half * HALF, (half + 1) * HALF)
                dve.tensor_tensor(xt_lo[:, h, ks, :], aux[:, c0:c0 + BANK].rearrange("p (k i) -> p k i", k=HALF),
                                  xt_hi[:, h, ks, :].bitcast(F32), ALU.subtract).then_inc(x_split, 1)

            x_low(0, 0, 0)
            x_low(0, 0, 1, BANK)
            turn(2)
            dve.wait_ge(h_ready, 4 * KT)
            for h in range(2):
                dve.tensor_copy(sel_lo[:, h, :, 0:NR], h_lo[:, :, C_H:C_LOW2]).then_inc(sel_fixed, 1)
            dve.wait_ge(vb_hd, 2)
            dve.tensor_tensor(c_lo[:], bp[0:R, C_LOW2:C_ALL], c_hi[:].bitcast(F32), ALU.subtract).then_inc(vb_done, 1)
            dve.tensor_tensor(vb_lo[:], bp[:, 0:C_LOW2], vb_hi[:].bitcast(F32), ALU.subtract).then_inc(vb_done, 1)
            link(dve.memset(v_sb[:], 0.0))

            def tile(t, b, h, finish, ahead):
                s = 1 - h
                if finish:
                    dve.wait_ge(main_done, t)
                    dve.tensor_copy(v_sb[:, 0:2 * R], acc[:, s, V0:V0 + 2 * R]).then_inc(v_out, 1)
                    dve.wait_ge(v_hd, t)
                    dve.tensor_tensor(vt_l[:], aux[0:2 * R, BANK:BANK + P], vt_h[:].bitcast(F32),
                                      ALU.subtract).then_inc(v_split, 1)
                if ahead:
                    x_low(t + 1, s, 0)
                if finish:
                    dve.wait_ge(m_hd, t)
                    dve.tensor_tensor(vm_l[:], aux[0:2 * R, BANK + P:BANK + 2 * P], vm_h[:].bitcast(F32),
                                      ALU.subtract).then_inc(m_split, 1)
                    lg, top, idx, g0, g1 = (gate[:, 8 * n:8 * n + 8] for n in (0, 1, 2, 4, 5))
                    link.n = t * GLINKS + (base - GLINKS)
                    dve.wait_ge(r_done, t)
                    link(dve.tensor_tensor(lg, acc[:, s, C_LOGIT:C_LOW2], bias7[:, b - 1 + h, :], ALU.add))
                    dve.sem_inc(logits_seen, 1)
                    link(dve.max(top, lg))
                    dve.tensor_tensor(gate[:, 25:26], gate[:, 9:10], gate[:, 8:9], ALU.subtract).then_inc(d_ready, 1)
                    link(dve.max_index(top_i[:], top, lg))
                    link(dve.tensor_copy(idx[:, 0:2], top_i[:, 0:2]))
                    dve.wait_ge(e_ready, t)
                    link(dve.tensor_scalar(gate[:, 26:27], gate[:, 24:25], 1.0, 0.5, ALU.add, ALU.mult))
                    link(dve.reciprocal(gate[:, 27:28], gate[:, 26:27]))
                    link(dve.tensor_scalar(gate[:, 28:29], gate[:, 27:28], gate[:, 24:25], None, ALU.mult))
                    link(dve.tensor_scalar(g0, iota_f[:], idx[:, 0:1], gate[:, 27:28], ALU.is_equal, ALU.mult))
                    link(dve.tensor_scalar(g1, iota_f[:], idx[:, 1:2], gate[:, 28:29], ALU.is_equal, ALU.mult))
                    link(dve.tensor_tensor(g0, g0, g1, ALU.add))
                    dve.tensor_tensor(hg[:], acc[:, s, C_H:C_LOGIT].rearrange("p (e r) -> p e r", e=E),
                                      g0.unsqueeze(2).to_broadcast([P, E, RE]), ALU.mult).then_inc(hg_ready, 1)
                if ahead:
                    x_low(t + 1, s, 1)
                if finish:
                    dve.wait_ge(g_hd, t)
                    dve.tensor_tensor(hgt_l[:], aux[:, BANK + 2 * P:BANK + 3 * P], hgt_h[:].bitcast(F32),
                                      ALU.subtract).then_inc(g_split, 1)
                    dve.wait_ge(o_done, t)
                    dve.wait_ge(out_done[s], (b + h) * 16)
                    dve.tensor_copy(out_sb[:, s, BANK:D], acc[:, s, BANK:D]).then_inc(o_dve, 1)

            base = link.n

            tile_schedule(dve, tile)

        @block.tensor
        def _(pe):
            def turn_tile(dst, src, **kw):
                return pe.transpose(dst, src, ident[0:src.shape[0], 0:src.shape[0]])

            pe.wait_ge(made, 2)
            pe.wait_ge(a3_in, 32)
            for k in range(KT):
                pe.wait_ge(w3_eye, k + 1)
                if k >= 2:
                    pe.wait_ge(h_ready, k - 1)
                for n in range(KT):
                    turn_tile(acc[:, k % 2, n * P:(n + 1) * P], g[:, n, k * P:(k + 1) * P])
                turn_tile(acc[:, k % 2, C_H:C_LOGIT], w1_eff[:, 0, k, :])
                turn_tile(acc[:, k % 2, C_LOGIT:C_LOW2], w1_eff[0:E, 1, k, :]).then_inc(w3_t, 1)
            pe.wait_ge(bank_in, 64)
            b1 = w1_eff[:, 2, 0:HALF].rearrange("p k i -> p (k i)").rearrange("p (k r) -> p k r", r=R1)
            for k in range(KT):
                last = turn_tile(aux[0:R1, k * P:(k + 1) * P], b1[:, k, :])
            last.then_inc(b1_t, 1)

            def delta(m):
                pe.wait_ge(aux_free, m + 1)
                for k in range(KT):
                    last = pe.matmul(aux[:, k * P:(k + 1) * P], b1t[:, k * P:(k + 1) * P],
                                     a1[:, bass.ds(m * P, P)], start=True, stop=True)
                last.then_inc(ld_done, 1)

            def one_pass(j, slot, w_h, w_l, rows):
                width = W_IN[j]
                for k in range(KT):
                    pe.wait_ge(h_ready, KT * j + k + 1)
                    for n, (a, b) in enumerate(((w_h, h_hi), (w_h, h_lo), (w_l, h_hi))):
                        for bank, (c0, c1) in enumerate(thirds(width)):
                            last = pe.matmul(acc[0:rows, slot, bank * BANK:bank * BANK + c1 - c0],
                                             a[:, k, :], b[:, k, c0:c1],
                                             start=(k == 0 and n == 0), stop=(k == KT - 1 and n == 2))
                    last.then_inc(h_used if k < KT - 1 else acc_done, 1)

            def step(j, m, h):
                pe.wait_ge(w_split, m + (KT * j + 1))
                pe.wait_ge(acc_free, m + (STEP0[j] + 1))
                one_pass(j, (STEP0[j] + h) % 2, w_hi[:, h], w_lo[:, h], P)

            pe.wait_ge(h_ready, KT)
            step(0, 0, 0)
            delta(0)
            step(0, 1, 1)
            with pe.Fori(1, KT // 2) as i:
                delta(i)
                for h in range(2):
                    step(0, i * 2 + h, h)
            pe.wait_ge(b_split, 2)
            pe.wait_ge(acc_free, KT + 1)
            one_pass(0, 0, b2h, b2l, R)
            for m in range(2):
                delta(m + 4)
                step(1, m, m)
            with pe.Fori(1, KT // 2 - 1) as i:
                step(1, i * 2, 0)
                delta(i + 5)
                step(1, i * 2 + 1, 1)
            for m in (6, 7):
                step(1, m, m % 2)
            with pe.Fori(0, KT // 2 - 1) as i:
                for h in range(2):
                    step(2, i * 2 + h, h)
            pe.wait_ge(b3_in, 16 * E)
            pe.wait_ge(aux_free, KT + 1)
            for k in range(KT):
                last = turn_tile(aux[:, k * P:(k + 1) * P], b3_raw[:, k].rearrange("p e r -> p (e r)"))
            last.then_inc(b3_t, 1)
            for m in (6, 7):
                step(2, m, m % 2)

            def x_turn(t, h, half, load, c0=0):
                pe.wait_ge(x_in[h], 16 * load)
                if c0 == 0 and (not isinstance(t, int) or t):
                    pe.wait_ge(x_split, t * 2 + half)
                for k in range(HALF):
                    kk = half * HALF + k
                    last = turn_tile(aux[:, c0 + k * P:c0 + (k + 1) * P], x_st[:, h, kk * P:(kk + 1) * P])
                last.then_inc(x_tr, 1)

            pe.wait_ge(b3_done, 1)
            x_turn(0, 0, 0, 1)
            x_turn(0, 0, 1, 1, BANK)
            pe.wait_ge(acc_free, PASSES)
            one_pass(2, 1, b0h, b0l, R)

            def three(dst, a, b, start=False, stop=False, **kw):
                (ah, al), (bh, bl) = a, b
                for n, (p, q) in enumerate(((ah, bh), (ah, bl), (al, bh))):
                    last = pe.matmul(dst, p, q, start=start and n == 0, stop=stop and n == 2, skip_group_check=True)
                return last

            def tile(t, b, h, finish, ahead):
                s = 1 - h

                def big(k):
                    for n, (a, b) in enumerate(((xt_hi, h_hi), (xt_hi, h_lo), (xt_lo, h_hi))):
                        for c0, c1 in chunks(D):
                            pe.matmul(acc[:, h, c0:c1], a[:, h, k, :], b[:, k, c0:c1],
                                      start=(k == 0 and n == 0), stop=False, skip_group_check=True)

                def small(k):
                    for n, (a, c) in enumerate(((xt_hi, sel_hi), (xt_hi, sel_lo), (xt_lo, sel_hi))):
                        last = pe.matmul(acc[:, h, C_H:V0 + 2 * R], a[:, h, k, :], c[:, h, k, :],
                                         start=(k == 0 and n == 0), stop=False, skip_group_check=True)
                    return last

                if ahead is not None:
                    pe.wait_ge(x_split, t * 2 + 2)
                    if finish:
                        if not isinstance(t, int) or t >= 2:
                            pe.wait_ge(o_act, t - 1)
                            pe.wait_ge(o_dve, t - 1)
                            pe.wait_ge(hg_ready, t - 1)
                for k in range(KT):
                    if ahead is not None:
                        if not finish:
                            pe.wait_ge(h_ready, 3 * KT + k + 1)
                        big(k)
                        if finish:
                            if k == 0:
                                pe.wait_ge(sel_ready, t * SELS + SELS)
                            last = small(k)
                    if finish and k == 0:
                        pe.wait_ge(v_out, t)
                        turn_tile(aux[:, BANK:BANK + P], v_sb[:]).then_inc(v_tr, 1)
                    if ahead and k == 1:
                        x_turn(t + 1, s, 0, b + 1 + h)
                    if finish and k == 2:
                        pe.wait_ge(v_split, t)
                        pe.wait_ge(tsel_ready, t * 2)
                        three(aux[:, BANK + P:BANK + 2 * P], (tsel_h[:, s], tsel_l[:, s]), (vt_h[:], vt_l[:]),
                              True, True).then_inc(mix_done, 1)
                    if finish and k == 3:
                        pe.wait_ge(m_split, t)
                        three(acc[:, s, C_H:C_LOW2], (vm_h[:], vm_l[:]),
                              (vb_hi[:, C_H:C_LOW2], vb_lo[:, C_H:C_LOW2]), stop=True).then_inc(r_done, 1)
                        for c0, c1 in chunks(D):
                            three(acc[:, s, c0:c1], (vm_h[:], vm_l[:]), (vb_hi[:, c0:c1], vb_lo[:, c0:c1]))
                    if ahead and k == 4:
                        x_turn(t + 1, s, 1, b + 1 + h)
                    if finish and k == 5:
                        pe.wait_ge(hg_ready, t)
                        turn_tile(aux[:, BANK + 2 * P:BANK + 3 * P],
                                  hg[:].rearrange("p e r -> p (e r)")).then_inc(g_tr, 1)
                    if finish and k == 6:
                        pe.wait_ge(g_split, t)
                        for c0, c1 in chunks(D):
                            done = three(acc[:, s, c0:c1], (hgt_h[:], hgt_l[:]), (b3_hi[:, c0:c1], b3_lo[:, c0:c1]),
                                         stop=True)
                        done.then_inc(o_done, 1)
                if ahead is not None:
                    if not finish:
                        pe.wait_ge(sel_fixed, 4)
                        pe.wait_ge(sel_ready, SELS)
                        for k in range(KT):
                            last = small(k)
                    last.then_inc(main_done, 1)

            tile_schedule(pe, tile)
    return nc


_INS = ['x', 'itok_B_0_4', 'condB_codebook', 'itok_B_0_2', 'itok_B_0_7', 'L0_cond_weight', 'L0_cond_lora_A',
        'L0_cond_lora_B_w', 'L1_cond_weight', 'L1_cond_scale_log', 'L1_cond_lora_A', 'L1_cond_lora_B',
        'L2_cond_W', 'L2_cond_lora_A', 'L2_cond_lora_B_w', 'L3_cond_W', 'L3_cond_Wr', 'L3_cond_A', 'L3_cond_B']


def kernel(**inputs):
    import numpy as _np
    import concourse.bacc as _bacc
    from concourse import mybir as _mybir
    from concourse.bass_utils import run_bass_kernel_spmd as _run

    nc = _bacc.Bacc("TRN2", target_bir_lowering=False, num_devices=1)
    arrays, args = {}, []
    for name in _INS:
        a = _np.ascontiguousarray(inputs[name])
        arrays[f"in_{name}_dram"] = a
        args.append(nc.dram_tensor(f"in_{name}_dram", a.shape, _mybir.dt.from_np(a.dtype), kind="ExternalInput").ap())
    shape = inputs['x'].shape
    args.append(nc.dram_tensor("out_0_dram", shape, _mybir.dt.float32, kind="ExternalOutput").ap())
    build(nc, *args)
    r = _run(nc, [arrays], core_ids=[0])
    return r.results[0]["out_0_dram"]
```

```python
from contextlib import ExitStack
from math import factorial

import concourse.bass as bass
from concourse import mybir

ALU = mybir.AluOpType
ACT = mybir.ActivationFunctionType
AX = mybir.AxisListType
F32 = mybir.dt.float32
F32R = mybir.dt.float32r
I32 = mybir.dt.int32
U32 = mybir.dt.uint32

P = 128
LOG2E = 1.4426950408889634
LN2_HIGH = 0.693359375
LN2_LOW = -2.12194440054690583e-4
ROUND = 1.5 * (1 << 23)
EXP_TERMS = 8
EXP_LOW, EXP_HIGH = -87.0, 88.0
BANK = 512


class Chain:

    def __init__(self, eng, sem):
        self.eng, self.sem, self.n = eng, sem, 0

    def __call__(self, instruction):
        instruction.then_inc(self.sem, 1)
        self.n = self.n + 1
        self.eng.wait_ge(self.sem, self.n)


def build(nc, x, lab0, codebook, lab2, lab7, W0, A0, B0, W1, scale_log, A1, B1, W2, A2, B2, W3, Wr, A3, B3, out):
    BATCH, SEQ, D = x.shape
    LABELS, _, R = A0.shape
    R1 = A1.shape[0]
    E, RE, _ = A3.shape
    ER = E * RE
    KT = D // P
    G1 = scale_log.shape[1]
    LEVELS = codebook.shape[0]
    TILES = BATCH * SEQ // P
    PER_BATCH = SEQ // P
    C_H, C_LOGIT, C_LOW2 = D, D + ER, D + ER + E
    C_ALL = C_LOW2 + LABELS * R
    NR = ER + E
    assert (D, PER_BATCH, D // G1, ER, KT, LEVELS, R1, R) == (1024, 2, P, P, 8, 8, 64, 32)
    W_IN = (C_LOW2, C_ALL, C_ALL)
    W_OUT = (C_ALL, C_ALL, C_LOW2)
    STEP0 = (0, KT + 1, 2 * KT + 1)
    PASSES = 3 * KT + 2
    HALF = KT // 2
    OFF = 2 * R
    SEL = (0, OFF + C_LOW2)
    W_TILE = C_LOW2 + 2 * R
    PART = W_TILE // 3

    SLOTS = 4
    QUANT = ({0: [(0, 0)], 1: [(0, 1), (0, 2)], 2: [(1, 0), (1, 1)], 3: [(1, 2), (2, 0)], 4: [(2, 1), (2, 2)],
              5: [(3, 0), (3, 1)], 6: [(3, 2), (4, 0)], 7: [(4, 1), (4, 2)]},
             {0: [(5, 0), (5, 1)], 1: [(5, 2), (6, 0)], 2: [(6, 1), (6, 2)], 3: [(7, 0), (7, 1)], 4: [(7, 2)]})
    FIRST_PART = [{m: n for m, parts in q.items() for n, part in parts if part == 0} for q in QUANT]
    LAST_PART = [{m: n for m, parts in q.items() for n, part in parts if part == 2} for q in QUANT]
    Q = 32
    QUARTERS = P // Q

    def thirds(width):
        part = -(-width // 6) * 2
        return [(n * part, min(width, (n + 1) * part)) for n in range(3)]

    with ExitStack() as ctx:
        def sb(name, shape, dt=F32, stack=ctx):
            return stack.enter_context(nc.sbuf_tensor(name, shape, dt))

        def sem(name):
            return ctx.enter_context(nc.semaphore(name))

        h_hi = sb("h_hi", [P, KT, OFF + C_ALL], F32R)
        h_lo = sb("h_lo", [P, KT, OFF + C_ALL], F32R)
        ident = sb("ident", [P, P])
        bp = sb("bp", [2 * R, C_ALL])
        b2raw, b0raw = sb("b2raw", [P, KT, R]), sb("b0raw", [P, KT, R])
        b2s, b0s = sb("b2s", [P, KT, 2 * R], F32R), sb("b0s", [P, KT, 2 * R], F32R)
        scale, rscale = sb("scale", [P, KT, G1]), sb("rscale", [P, KT, G1])
        exp_t, exp_n = sb("exp_t", [P, 2, KT, G1]), sb("exp_n", [P, KT, G1], I32)
        book = sb("book", [P, LEVELS])
        steps = sb("steps", [P, LEVELS])
        thr = sb("thr", [P, LEVELS])
        tmp8 = sb("tmp8", [P, 2 * LEVELS])
        labi = sb("labi", [1, 2 * BATCH], I32)
        labf = sb("labf", [1, 4 * BATCH])
        labu = sb("labu", [1, 2 * BATCH], I32)
        lab7i = sb("lab7i", [P, BATCH], I32)
        lab7f = sb("lab7f", [P, BATCH])
        iota_i = sb("iota_i", [P, E], I32)
        iota_f = sb("iota_f", [P, E])
        bias7 = sb("bias7", [P, BATCH, E])

        first = ExitStack()
        g = sb("g", [P, KT, C_ALL], F32, first)
        w1_st = sb("w1_st", [P, 2, KT, P], F32, first)
        w1_eff = sb("w1_eff", [P, SLOTS, KT, P], F32, first)
        ldelta = sb("ldelta", [P, KT, P], F32, first)
        qtmp = sb("qtmp", [P, KT, P], F32, first)
        a1 = sb("a1", [R1, D], F32, first)
        b1t = sb("b1t", [R1, D], F32, first)
        w_hi = sb("w_hi", [P, 2, KT, P], F32R, first)
        w_lo = sb("w_lo", [P, 2, KT, P], F32R, first)
        w_st = sb("w_st", [P, 2, KT, P], F32, first)
        first.close()
        vb_hi, vb_lo = sb("vb_hi", [P, C_LOW2], F32R), sb("vb_lo", [2 * R, C_LOW2], F32R)
        c_hi, c_lo = sb("c_hi", [P, LABELS * R], F32R), sb("c_lo", [2 * R, LABELS * R], F32R)
        out_sb = sb("out_sb", [P, 2, D])
        v_sb = sb("v_sb", [P, 2, 2 * R])
        vt = sb("vt", [P, P], F32R)
        vm = sb("vm", [P, P], F32R)
        hg = sb("hg", [P, E, RE])
        hgt_h, hgt_l = sb("hgt_h", [P, P], F32R), sb("hgt_l", [P, P], F32R)
        gate = sb("gate", [P, 96])
        top_i = sb("top_i", [P, 8], U32)
        used = 2 * C_LOW2 + 2 * LABELS * R + 2 * D + P + 2 * P + P + 2 * P + 96 + 8
        sb("pad", [P, KT * C_ALL - used])
        a0_raw = sb("a0_raw", [P, KT, LABELS * R])
        a0_hi, a0_lo = sb("a0_hi", [P, KT, LABELS * R], F32R), sb("a0_lo", [P, KT, LABELS * R], F32R)
        b3_raw = sb("b3_raw", [P, KT, E, RE])
        b3_hi, b3_lo = sb("b3_hi", [P, D], F32R), sb("b3_lo", [P, D], F32R)
        low_hi, low_lo = sb("low_hi", [P, KT, LABELS * R], F32R), sb("low_lo", [P, KT, LABELS * R], F32R)
        tsel_h, tsel_l = sb("tsel_h", [P, 2, P], F32R), sb("tsel_l", [2 * R, 2, P], F32R)
        sb("pad2", [P, (6 + SLOTS) * D - 5 * KT * LABELS * R - 3 * D - 4 * P])
        xt = b3_raw[:].rearrange("p k e r -> p k (e r)")
        xt_hi, xt_lo = sb("xt_hi", [P, 2, KT, P], F32R), sb("xt_lo", [P, 2, KT, P], F32R)
        x_st = sb("x_st", [P, 2, D])

        acc = ctx.enter_context(nc.psum_tensor("acc", [P, 2, 3 * BANK], F32))
        aux = ctx.enter_context(nc.psum_tensor("aux", [P, 2 * BANK], F32))

        def in_banks(slot, h, c0, c1):
            lead = (OFF, 0)[h]
            for bank in range(3):
                a, b = max(c0, bank * PART - lead), min(c1, (bank + 1) * PART - lead)
                if a < b:
                    at = bank * BANK + a + lead - bank * PART
                    yield acc[:, slot, at:at + b - a], a, b

        def in_bank(slot, h, c0, c1):
            (where, _, _), = in_banks(slot, h, c0, c1)
            return where

        def v_columns(slot):
            return acc[:, slot, 0:2 * R] if slot == 0 else in_bank(slot, 1, C_LOW2, W_TILE)

        w3_in = [sem(f"w3_in{k}") for k in range(KT)]
        small_in, tables_in, a3_in, a2_in = sem("small_in"), sem("tables_in"), sem("a3_in"), sem("a2_in")
        w_in = [sem(f"w_in{i}") for i in range(2)]
        w1_in = sem("w1_in")
        a0_in, b3_in = sem("a0_in"), sem("b3_in")
        x_in = [sem(f"x_in{i}") for i in range(2)]
        out_done = [sem(f"out_done{i}") for i in range(2)]
        made = sem("made")
        w3_eye = sem("w3_eye")
        w3_t = sem("w3_t")
        a3_t = sem("a3_t")
        a3_hd, a3_done = sem("a3_hd"), sem("a3_done")
        split_hi = sem("split_hi")
        h_ready = sem("h_ready")
        h_used = sem("h_used")
        acc_done = sem("acc_done")
        acc_free = sem("acc_free")
        acc_part = sem("acc_part")
        w_eye = sem("w_eye")
        w_hi_done = sem("w_hi_done")
        w_split = sem("w_split")
        b_hi, b_split = sem("b_hi"), sem("b_split")
        b1_t = sem("b1_t")
        tables = sem("tables")
        ld_done = sem("ld_done")
        aux_free = sem("aux_free")
        v_ready = sem("v_ready")
        q_ready = sem("q_ready")
        q_sum, w1e_done = sem("q_sum"), sem("w1e_done")
        dve_chain = sem("dve_chain")
        a0_hd, a0_done = sem("a0_hd"), sem("a0_done")
        b3_t, b3_hd, b3_done = sem("b3_t"), sem("b3_hd"), sem("b3_done")
        bp_part = sem("bp_part")
        bp_added = sem("bp_added")
        vb_hd, vb_done = sem("vb_hd"), sem("vb_done")
        zeroed, eyed = sem("zeroed"), sem("eyed")
        x_tr, x_hd, x_split = sem("x_tr"), sem("x_hd"), sem("x_split")
        x_seen = sem("x_seen")
        low_hd, low_done = sem("low_hd"), sem("low_done")
        sel_ready = sem("sel_ready")
        tsel_ready = sem("tsel_ready")
        main_done = sem("main_done")
        v_out, v_tr, v_hd, v_split = sem("v_out"), sem("v_tr"), sem("v_hd"), sem("v_split")
        mix_done, m_hd, m_split = sem("mix_done"), sem("m_hd"), sem("m_split")
        logits_seen, room_seen = sem("logits_seen"), sem("room_seen")
        r_done = sem("r_done")
        d_ready, e_ready = sem("d_ready"), sem("e_ready")
        hg_ready, g_tr, g_hd, g_split = sem("hg_ready"), sem("g_tr"), sem("g_hd"), sem("g_split")
        o_done, o_dve = sem("o_done"), sem("o_dve")
        o_act = [sem(f"o_act{bank}") for bank in range(2)]

        GLINKS = 10
        SELS = 4

        x_rows = x.rearrange("b s d -> (b s) d")
        out_rows = out.rearrange("b s d -> (b s) d")

        def slices(w):
            return w.rearrange("(k p) i -> p k i", p=P)

        def wait_tile_used(eng, j, k):
            last = STEP0[j] + KT - 1 + (j != 1)
            if k < KT - 1:
                eng.wait_ge(h_used, (KT - 1) * last + k + 1)
            else:
                eng.wait_ge(acc_done, last + 1)

        def tile_schedule(eng, tile):
            tile(0, 0, 0, False, True)
            tile(1, 0, 1, True, True)
            with eng.Fori(1, BATCH - 1) as b:
                for h in range(2):
                    tile(b * 2 + h, b, h, True, True)
            tile(TILES - 2, BATCH - 1, 0, True, True)
            tile(TILES - 1, BATCH - 1, 1, True, False)
            tile(TILES, BATCH, 0, True, None)

        a3_tiles = [(k, min(KT, k + 3)) for k in range(0, KT, 3)]

        def w3_at(k):
            return acc[:, 1, 0:D] if k % 2 else aux[:, :]

        def a3_at(bank, k0, k1):
            return acc[:, 0, bank * BANK:bank * BANK + (k1 - k0) * NR].rearrange("p (k c) -> p k c", k=k1 - k0)

        block = ctx.enter_context(nc.Block())

        @block.sync
        def _(sp):
            for h in range(2):
                sp.sem_inc(out_done[h], 16)
            for k in range(KT):
                sp.dma_start(g[:, :, k * P:(k + 1) * P], slices(W3)[:, :, k * P:(k + 1) * P]).then_inc(w3_in[k], 16)
                if k == 0:
                    sp.dma_start(w1_eff[:, 0].rearrange("p k i -> p (k i)"),
                                 A3.rearrange("e r d -> (e r) d")).then_inc(a3_in, 16)
                    sp.dma_start(w1_eff[0:E, 1].rearrange("p k i -> p (k i)"), Wr).then_inc(a3_in, 16)
                    sp.dma_start(w_st[:, 0], slices(W2)[:, :, 0:P]).then_inc(w_in[0], 16)
            sp.dma_start(w_st[:, 1], slices(W2)[:, :, P:2 * P]).then_inc(w_in[1], 16)
            sp.dma_start(book[:], codebook.rearrange("(a c) -> a c", a=1).to_broadcast([P, LEVELS])).then_inc(tables_in, 16)
            sp.dma_start(scale[:], scale_log.rearrange("(k p) g a -> p k (g a)", p=P)).then_inc(tables_in, 16)
            sp.dma_start(w1_eff[:, 2, 0:HALF].rearrange("p k i -> p (k i)").rearrange("p (k r) -> p k r", r=R1),
                         B1.rearrange("(k p) r -> p k r", p=P)).then_inc(tables_in, 16)
            sp.dma_start(a1[:], A1).then_inc(tables_in, 16)
            sp.dma_start(w1_st[:, 0], slices(W1)[:, :, 0:P]).then_inc(w1_in, 16)
            sp.dma_start(labi[0:1, 0:BATCH], lab0.rearrange("(a c) -> a c", a=1)).then_inc(small_in, 16)
            sp.dma_start(labi[0:1, BATCH:], lab2.rearrange("(a c) -> a c", a=1)).then_inc(small_in, 16)
            sp.dma_start(lab7i[:], lab7.rearrange("(a c) -> a c", a=1).to_broadcast([P, BATCH])).then_inc(small_in, 16)
            sp.dma_start(b2raw[:], B2.rearrange("(k p) r -> p k r", p=P)).then_inc(small_in, 16)
            sp.dma_start(b0raw[:], B0.rearrange("(k p) r -> p k r", p=P)).then_inc(small_in, 16)
            for l in range(LABELS):
                sp.dma_start(g[:, :, C_LOW2 + l * R:C_LOW2 + (l + 1) * R],
                             A2[l].rearrange("(k p) r -> p k r", p=P)).then_inc(a2_in, 16)

            def load_w(W, h, cols, need):
                sp.wait_ge(w_split, need)
                sp.dma_start(w_st[:, h], slices(W)[:, :, cols]).then_inc(w_in[h], 16)

            def load_w0(h, m, need):
                sp.wait_ge(w_split, need)
                for a in range(QUARTERS):
                    sp.dma_start(w_st[:, h, :, a * Q:(a + 1) * Q],
                                 slices(W0)[:, :, bass.ds(m * Q + a * (D // QUARTERS), Q)]).then_inc(w_in[h], 16)

            def load_w1(n, h):
                sp.wait_ge(q_ready, n - 1)
                sp.wait_ge(w1_in, n * 16)
                sp.dma_start(w1_st[:, h], slices(W1)[:, :, bass.ds(n * P, P)]).then_inc(w1_in, 16)

            sp.wait_ge(w1_in, 16)
            sp.dma_start(w1_st[:, 1], slices(W1)[:, :, P:2 * P]).then_inc(w1_in, 16)
            for h in range(2):
                load_w(W2, h, bass.ds((2 + h) * P, P), h + 1)
            for m in range(KT - 2):
                if m < KT - 4:
                    load_w(W2, m % 2, bass.ds((m + 4) * P, P), m + 3)
                else:
                    load_w0(m % 2, m + 4 - KT, m + 3)
                if (n := LAST_PART[0].get(m)) is not None:
                    load_w1(n + 2, n % 2)
            for n in range(5, KT):
                load_w1(n, n % 2)
            sp.wait_ge(w_split, 2 * KT)
            for l in range(LABELS):
                for a in range(QUARTERS):
                    sp.dma_start(a0_raw[a * Q:(a + 1) * Q, :, l * R:(l + 1) * R],
                                 A0[l].rearrange("(a k q) r -> a q k r", a=QUARTERS, q=Q)[a]).then_inc(a0_in, 16)
            with sp.Fori(0, KT // 2 - 1) as i:
                for h in range(2):
                    m = i * 2 + h
                    load_w0(h, m + 2, m + 2 * KT + 1)
            for e in range(E):
                sp.dma_start(b3_raw[:, :, e], B3[e].rearrange("(k p) r -> p k r", p=P)).then_inc(b3_in, 16)

            sp.wait_ge(w_split, 3 * KT)
            def load_x(h, row):
                for a in range(QUARTERS):
                    f0 = a * (D // QUARTERS)
                    sp.dma_start(x_st[a * Q:(a + 1) * Q, h].rearrange("r (c f) -> r c f", c=QUARTERS),
                                 x_rows[bass.ds(row, P), f0:f0 + D // QUARTERS].rearrange("(c r) f -> r c f", r=Q)
                                 ).then_inc(x_in[h], 16)

            for t in range(2):
                load_x(t, t * P)

            def tile_io(t, h, load, store):
                if load:
                    sp.wait_ge(x_tr, t * 2 + 2)
                    load_x(h, t * P + 2 * P)
                if store:
                    for bank in range(2):
                        sp.wait_ge(o_act[bank], t + 1)
                    sp.wait_ge(o_dve, t + 1)
                    sp.dma_start(out_rows[bass.ds(t * P, P), :], out_sb[:, h]).then_inc(out_done[h], 16)

            tile_io(0, 0, True, False)
            tile_io(1, 1, True, False)
            with sp.Fori(0, TILES // 2 - 2) as i:
                for h in range(2):
                    t = i * 2 + h
                    tile_io(t + 2, h, True, False)
                    tile_io(t, h, False, True)
            for t in range(TILES - 4, TILES):
                tile_io(t, t % 2, False, True)
            for h in range(2):
                sp.wait_ge(out_done[h], 16 * (TILES // 2 + 1))

        @block.gpsimd
        def _(pool):
            def add_eye(tile, m):
                return pool.tensor_tensor(tile[:, m, :], tile[:, m, :], ident[:], ALU.add)

            pool.sem_inc(q_sum, 1)
            pool.memset(ident[:], 0.0).then_inc(made, 1)
            pool.wait_ge(made, 1)
            pool.affine_select(out=ident[:], in_=ident[:], compare_op=ALU.not_equal, fill=1.0, base=0,
                               pattern=[[-1, P]], channel_multiplier=1).then_inc(made, 1)
            pool.iota(iota_i[:], pattern=[[1, E]], base=0, channel_multiplier=0).then_inc(made, 1)
            pool.wait_ge(made, 3)

            def eye_w(h, m, load):
                pool.wait_ge(w_in[h], 16 * load)
                add_eye(w_st[:, h], m).then_inc(w_eye, 1)

            def eye_w0(h, m):
                pool.wait_ge(w_in[h], 16 * (HALF + QUARTERS * (m // 2 + 1)))
                for a in range(QUARTERS):
                    k, row = divmod(a * (D // QUARTERS) + m * Q, P)
                    at = w_st[:, h, k, a * Q:(a + 1) * Q]
                    pool.tensor_tensor(at, at, ident[:, row:row + Q], ALU.add).then_inc(w_eye, 1)

            for k in range(KT):
                pool.wait_ge(w3_in[k], 16)
                add_eye(g[:, :, k * P:(k + 1) * P], k).then_inc(w3_eye, 1)
                if k == 0:
                    eye_w(0, 0, 1)

            def quant_out(m, slot):
                pool.wait_ge(q_ready, m + 1)
                pool.wait_ge(aux_free, m + 2)
                pool.tensor_tensor(w1_eff[:, slot], w1_eff[:, slot], ldelta[:], ALU.add).then_inc(q_sum, 1)
                pool.wait_ge(q_sum, m + 2)
                add_eye(w1_eff[:, slot], m).then_inc(w1e_done, 1)

            eye_w(1, 1, 1)
            eye_w(0, 2, 2)
            for m in range(KT):
                n = LAST_PART[0].get(m)
                if m + 3 < KT:
                    eye_w((m + 1) % 2, m + 3, (m + 1) // 2 + 2)
                elif m + 1 < KT:
                    eye_w0((m + 1) % 2, m + 3 - KT)
                if n is not None:
                    quant_out(n, n % SLOTS)
            for n in LAST_PART[1].values():
                quant_out(n, n % SLOTS)
            for m in range(2, KT):
                eye_w0(m % 2, m)

            def label(which, b):
                return pool.value_load(labu[0:1, bass.ds(b + which * BATCH, 1)], min_val=0, max_val=LABELS - 1)

            def select(h, c, label_, parts):
                for dst, src in zip((h_hi, h_lo), parts):
                    pool.tensor_copy(dst[:, :, SEL[h] + c:SEL[h] + c + R],
                                     src[:, :, bass.ds(label_ * R, R)]).then_inc(sel_ready, 1)

            def select_both(h, l0, l2):
                select(h, 0, l0, (a0_hi, a0_lo))
                select(h, R, l2, (low_hi, low_lo))

            def twice(ap, rows):
                return ap.unsqueeze(1).to_broadcast([rows, 2, ap.shape[-1]])

            def mixer(l2, h):
                for ts, c, rows in ((tsel_h, c_hi, P), (tsel_l, c_lo, 2 * R)):
                    pool.tensor_copy(ts[0:rows, h].rearrange("p (u c) -> p u c", u=2)[:, :, R:2 * R],
                                     twice(c[0:rows, bass.ds(l2 * R, R)], rows)).then_inc(tsel_ready, 1)

            pool.wait_ge(w_split, 2 * KT)
            for n, ts in enumerate((tsel_h, tsel_l)):
                pool.memset(ts[:].bitcast(F32), 0.0).then_inc(zeroed, 1)
            pool.wait_ge(zeroed, 2)
            pool.wait_ge(w1e_done, KT)
            for n, (h, rows) in enumerate(((0, slice(0, 2 * R)), (1, slice(0, 2 * R)), (0, slice(2 * R, P)),
                                           (1, slice(2 * R, P)))):
                pool.tensor_copy(tsel_h[rows, h].rearrange("p (u c) -> p u c", u=2),
                                 twice(ident[rows, rows], 2 * R)).then_inc(eyed, 1)
                pool.wait_ge(eyed, n + 1)
            pool.wait_ge(tables, 2)
            first_l0, first_l2 = label(0, 0), label(1, 0)
            pool.wait_ge(a0_done, 1)
            select(0, 0, first_l0, (a0_hi, a0_lo))
            pool.wait_ge(low_done, 1)
            select(0, R, first_l2, (low_hi, low_lo))
            pool.wait_ge(h_ready, 4 * KT)
            select_both(1, first_l0, first_l2)
            pool.wait_ge(vb_done, 4)
            for h in range(2):
                mixer(first_l2, h)
            with pool.Fori(1, BATCH) as b:
                l0, l2 = label(0, b), label(1, b)
                for h in range(2):
                    pool.wait_ge(main_done, b * 2 + (h - 1))
                    pool.sem_inc(room_seen, 1)
                    select_both(h, l0, l2)
                    pool.wait_ge(mix_done, b * 2 + (h - 1))
                    pool.sem_inc(room_seen, 1)
                    mixer(l2, h)

        @block.scalar
        def _(act):
            act.sem_inc(acc_free, 2)
            for k in range(KT):
                act.wait_ge(w3_t, k + 1)
                act.copy(h_hi[:, k, OFF:OFF + D], w3_at(k)).then_inc(split_hi, 1)
                if k == 0:
                    act.wait_ge(w_eye, 1)
                    act.copy(w_hi[:, 0], w_st[:, 0]).then_inc(w_hi_done, 1)
                    act.wait_ge(a3_t, 1)
                    for bank, (k0, k1) in enumerate(a3_tiles):
                        act.copy(h_hi[:, k0:k1, OFF + C_H:OFF + C_LOW2], a3_at(bank, k0, k1)).then_inc(a3_hd, 1)
            act.wait_ge(w_eye, 2)
            act.copy(w_hi[:, 1], w_st[:, 1]).then_inc(w_hi_done, 1)
            act.wait_ge(b1_t, 1)
            act.mul(b1t[:], aux[0:R1, :], 0.5).then_inc(aux_free, 1)

            def high(src, h, ready, count):
                act.wait_ge(ready, count)
                act.copy(w_hi[:, h], src).then_inc(w_hi_done, 1)

            def copy_delta(m):
                act.wait_ge(ld_done, m + 1)
                act.wait_ge(v_ready, m + 1)
                act.wait_ge(q_sum, m + 1)
                act.copy(ldelta[:], aux[:, :].rearrange("p (k i) -> p k i", k=KT)).then_inc(aux_free, 1)

            def evacuate(dst, slot, row0, rows, width):
                parts = thirds(width)
                part = parts[0][1]
                banks = acc[row0:row0 + rows, slot, :].rearrange("p (n c) -> p n c", n=3)
                even = 3 if width == 3 * part else 2
                last = act.copy(dst[:, 0:even * part].rearrange("p (n c) -> p n c", n=even), banks[:, 0:even, 0:part])
                if even == 2:
                    last.then_inc(acc_part, 1)
                    last = act.copy(dst[:, 2 * part:width], banks[:, 2, 0:width - 2 * part])
                last.then_inc(acc_free, 1)

            def turn(j, k0=0, k1=KT):
                act.wait_ge(acc_free, 2 + STEP0[j] + min(k1, KT))
                if j == 0:
                    act.wait_ge(acc_part, KT)
                    act.wait_ge(a2_in, 16 * LABELS)
                for k in range(k0, k1):
                    wait_tile_used(act, j, k)
                    act.copy(h_hi[:, k, OFF:OFF + W_OUT[j]], g[:, k, 0:W_OUT[j]]).then_inc(split_hi, 1)

            act.wait_ge(small_in, 80)
            act.mul(b2s[:, :, 0:R], b2raw[:], 0.5).then_inc(b_hi, 1)
            act.mul(b0s[:, :, 0:R], b0raw[:], 0.5).then_inc(b_hi, 1)

            def step(j, m, h, src, ready, count, delta=None):
                if delta is not None:
                    copy_delta(delta)
                act.wait_ge(acc_done, m + (STEP0[j] + 1))
                if src is not None:
                    high(src, h, ready, count)
                evacuate(g[:, m, :], (STEP0[j] + h) % 2, 0, P, W_IN[j])

            for m in range(KT):
                src, ready, count = (w_st[:, m % 2], w_eye, m + 3) if m < KT - 2 else (w1_eff[:, m - 6], w1e_done, m - 5)
                step(0, m, m % 2, src, ready, count, delta=FIRST_PART[0].get(m - 1))
            turn(0)
            act.wait_ge(acc_done, KT + 1)
            evacuate(bp[R:2 * R, :], 0, 0, R, C_LOW2)
            for m in range(KT - 2):
                step(1, m, m % 2, w1_eff[:, (m + 2) % SLOTS], w1e_done, m + 3, delta=FIRST_PART[1].get(m - 1))
            step(1, 6, 0, w_st[:, 0], w_eye, KT + QUARTERS)
            turn(1, 0, KT - 1)
            step(1, 7, 1, w_st[:, 1], w_eye, KT + 2 * QUARTERS)
            turn(1, KT - 1, KT)
            act.wait_ge(a0_in, 16 * LABELS * QUARTERS)
            act.copy(a0_hi[:], a0_raw[:]).then_inc(a0_hd, 1)
            with act.Fori(0, KT // 2 - 1) as i:
                for h in range(2):
                    m = i * 2 + h
                    step(2, m, h, w_st[:, h], w_eye, m * QUARTERS + (KT + 3 * QUARTERS))
            act.wait_ge(b3_t, 1)
            act.copy(b3_hi[:], aux[:, :]).then_inc(b3_hd, 1)
            for m in (6, 7):
                step(2, m, m % 2, None, None, None)

            def x_high(t, h, half):
                act.wait_ge(x_tr, t * 2 + (half + 1))
                ks = slice(half * HALF, (half + 1) * HALF)
                act.copy(xt_hi[:, h, ks, :], xt[:, ks, :]).then_inc(x_hd, 1)

            x_high(0, 0, 0)
            x_high(0, 0, 1)
            act.wait_ge(acc_free, 2 + STEP0[2] + KT)
            act.copy(low_hi[:], g[:, :, C_LOW2:]).then_inc(low_hd, 1)
            turn(2)
            act.wait_ge(acc_done, PASSES)
            evacuate(bp[0:R, :], 1, R, R, C_ALL)

            def split_bp():
                act.wait_ge(bp_added, 2)
                act.wait_ge(h_ready, 4 * KT)
                for half in range(2):
                    act.copy(c_hi[half * 2 * R:half * 2 * R + R, :], bp[0:R, C_LOW2:C_ALL]).then_inc(vb_hd, 1)
                for half in range(2):
                    act.copy(vb_hi[half * 2 * R:(half + 1) * 2 * R, :], bp[:, 0:C_LOW2]).then_inc(vb_hd, 1)

            def tile(t, b, h, finish, ahead):
                if finish:
                    act.wait_ge(v_tr, t)
                    act.copy(vt[:], aux[:, BANK:BANK + P]).then_inc(v_hd, 1)
                if ahead:
                    if finish:
                        act.wait_ge(main_done, t)
                    x_high(t + 1, 1 - h, 0)
                if finish:
                    act.wait_ge(mix_done, t)
                    act.copy(vm[:], aux[:, BANK + P:BANK + 2 * P]).then_inc(m_hd, 1)
                    act.wait_ge(d_ready, t)
                    act.activation(gate[:, 24:25], gate[:, 25:26], ACT.Exp).then_inc(e_ready, 1)
                if ahead:
                    x_high(t + 1, 1 - h, 1)
                if not finish:
                    split_bp()
                if finish:
                    act.wait_ge(g_tr, t)
                    act.copy(hgt_h[:], aux[:, BANK + 2 * P:BANK + 3 * P]).then_inc(g_hd, 1)
                    act.wait_ge(o_done, t)
                    act.wait_ge(out_done[1 - h], (b + h) * 16)
                    for bank, (where, c0, c1) in enumerate(list(in_banks(1 - h, 1 - h, 0, D))[:2]):
                        act.copy(out_sb[:, 1 - h, c0:c1], where).then_inc(o_act[bank], 1)

            tile_schedule(act, tile)

        @block.vector
        def _(dve):
            link = Chain(dve, dve_chain)

            def low(src, h, count):
                dve.wait_ge(w_hi_done, count)
                dve.tensor_tensor(w_lo[:, h], src, w_hi[:, h].bitcast(F32), ALU.subtract).then_inc(w_split, 1)

            for k in range(KT):
                dve.wait_ge(split_hi, k + 1)
                dve.tensor_tensor(h_lo[:, k, OFF:OFF + D], w3_at(k), h_hi[:, k, OFF:OFF + D].bitcast(F32),
                                  ALU.subtract).then_inc(h_ready, 1)
                if k == 0:
                    low(w_st[:, 0], 0, 1)
                    for bank, (k0, k1) in enumerate(a3_tiles):
                        cols = slice(OFF + C_H, OFF + C_LOW2)
                        dve.wait_ge(a3_hd, bank + 1)
                        dve.tensor_tensor(h_lo[:, k0:k1, cols], a3_at(bank, k0, k1), h_hi[:, k0:k1, cols].bitcast(F32),
                                          ALU.subtract).then_inc(a3_done, 1)

            low(w_st[:, 1], 1, 2)
            dve.wait_ge(tables_in, 64)
            link(dve.tensor_scalar(tmp8[:, 0:LEVELS], book[:], -1.0, None, ALU.mult))
            link(dve.tensor_tensor(tmp8[:, 0:LEVELS], tmp8[:, 0:LEVELS], book[:], ALU.max))
            link(dve.tensor_reduce(tmp8[:, 8:9], tmp8[:, 0:LEVELS], AX.X, ALU.max))
            link(dve.tensor_scalar(tmp8[:, 9:10], tmp8[:, 8:9], 1e-8, None, ALU.max))
            link(dve.reciprocal(tmp8[:, 10:11], tmp8[:, 9:10]))
            link(dve.tensor_scalar(book[:], book[:], tmp8[:, 10:11], None, ALU.mult))
            link(dve.tensor_tensor(thr[:, 0:7], book[:, 0:7], book[:, 1:8], ALU.add))
            link(dve.tensor_scalar(thr[:, 0:7], thr[:, 0:7], 0.5, None, ALU.mult))
            link(dve.tensor_tensor(steps[:, 0:7], book[:, 1:8], book[:, 0:7], ALU.subtract))

            def th(j):
                return thr[:, j:j + 1]
            link(dve.tensor_tensor(th(1), th(1), th(3), ALU.min))
            link(dve.tensor_tensor(th(5), th(5), th(3), ALU.max))
            link(dve.tensor_tensor(th(0), th(0), th(1), ALU.min))
            link(dve.tensor_tensor(th(6), th(6), th(5), ALU.max))
            link(dve.tensor_scalar(th(2), th(2), th(1), th(3), ALU.max, ALU.min))
            link(dve.tensor_scalar(th(4), th(4), th(3), th(5), ALU.max, ALU.min))
            xs, n_f, r_, p_ = scale[:], rscale[:], exp_t[:, 0], exp_t[:, 1]
            link(dve.tensor_scalar(xs, xs, EXP_LOW, EXP_HIGH, ALU.max, ALU.min))
            link(dve.tensor_scalar(n_f, xs, LOG2E, ROUND, ALU.mult, ALU.add))
            link(dve.tensor_scalar(n_f, n_f, ROUND, None, ALU.subtract))
            link(dve.scalar_tensor_tensor(out=r_, in0=n_f, scalar=-LN2_HIGH, in1=xs, op0=ALU.mult, op1=ALU.add))
            link(dve.scalar_tensor_tensor(out=r_, in0=n_f, scalar=-LN2_LOW, in1=r_, op0=ALU.mult, op1=ALU.add))
            link(dve.tensor_scalar(p_, r_, 1.0 / factorial(EXP_TERMS), None, ALU.mult))
            for d in range(EXP_TERMS - 1, 0, -1):
                link(dve.scalar_tensor_tensor(out=p_, in0=p_, scalar=1.0 / factorial(d), in1=r_,
                                              op0=ALU.add, op1=ALU.mult))
            link(dve.tensor_scalar(p_, p_, 1.0, None, ALU.add))
            link(dve.tensor_scalar(n_f, n_f, 127.0, float(1 << 23), ALU.add, ALU.mult))
            link(dve.tensor_copy(exp_n[:], n_f))
            link(dve.tensor_tensor(xs, p_, exp_n[:].bitcast(F32), ALU.mult))
            dve.reciprocal(rscale[:], xs).then_inc(tables, 1)

            def labels():
                dve.wait_ge(small_in, 80)
                nb = 2 * BATCH
                link(dve.tensor_copy(labf[:, 0:nb], labi[:]))
                link(dve.tensor_scalar(labf[:, nb:], labf[:, 0:nb], 0.0, float(LABELS), ALU.is_lt, ALU.mult))
                link(dve.tensor_tensor(labf[:, 0:nb], labf[:, 0:nb], labf[:, nb:], ALU.add))
                link(dve.tensor_scalar(labf[:, 0:nb], labf[:, 0:nb], 0.0, LABELS - 1.0, ALU.max, ALU.min))
                dve.tensor_copy(labu[:], labf[:, 0:nb]).then_inc(tables, 1)
                dve.wait_ge(made, 3)
                link(dve.tensor_copy(iota_f[:], iota_i[:]))
                link(dve.tensor_copy(lab7f[:], lab7i[:]))
                for b in range(BATCH):
                    last = dve.tensor_scalar(bias7[:, b, :], iota_f[:], lab7f[:, b:b + 1], 5.0, ALU.is_equal, ALU.mult)
                link(last)

            def split_b():
                for n, (raw, both) in enumerate(((b2raw, b2s), (b0raw, b0s))):
                    dve.wait_ge(b_hi, n + 1)
                    dve.scalar_tensor_tensor(out=both[:, :, R:], in0=raw[:], scalar=0.5, in1=both[:, :, 0:R].bitcast(F32),
                                             op0=ALU.mult, op1=ALU.subtract).then_inc(b_split, 1)

            def quantise(m, part):
                n = w1_st[:, m % 2]
                q = w1_eff[:, m % SLOTS]
                if part == 0:
                    dve.wait_ge(w1_in, 16 * (m + 1))
                    dve.wait_ge(ld_done, m + 1)
                    dve.tensor_tensor(n, n, aux[:, :].rearrange("p (k i) -> p k i", k=KT), ALU.add).then_inc(v_ready, 1)
                    dve.wait_ge(v_ready, m + 1)
                    link(dve.tensor_tensor(n, n, rscale[:, :, m:m + 1].to_broadcast([P, KT, P]), ALU.mult))
                    if m >= SLOTS:
                        dve.wait_ge(w_split, KT + m - SLOTS + 1)
                    link(dve.tensor_scalar(q, n, th(0), steps[:, 0:1], ALU.is_gt, ALU.mult))
                for j in ((1,), (2, 3, 4), (5, 6))[part]:
                    link(dve.tensor_scalar(qtmp[:], n, th(j), steps[:, j:j + 1], ALU.is_gt, ALU.mult))
                    link(dve.tensor_tensor(q, q, qtmp[:], ALU.add))
                if part == 2:
                    dve.scalar_tensor_tensor(out=q, in0=q, scalar=book[:, 0:1],
                                             in1=scale[:, :, m:m + 1].to_broadcast([P, KT, P]),
                                             op0=ALU.add, op1=ALU.mult).then_inc(q_ready, 1)

            def step(j, m, h, src, count):
                dve.wait_ge(acc_done, m + (STEP0[j] + 1))
                low(src, h, count)

            def add_bp(rows, slot, psum_rows, width):
                for bank, (c0, c1) in enumerate(thirds(width)):
                    last = dve.tensor_tensor(bp[rows, c0:c1], acc[psum_rows, slot, bank * BANK:bank * BANK + c1 - c0],
                                             bp[rows, c0:c1], ALU.add)
                    if bank < 2:
                        last.then_inc(bp_part, 1)
                last.then_inc(bp_added, 1)

            def turn(j, k0=0, k1=KT):
                for k in range(k0, k1):
                    wait_tile_used(dve, j, k)
                    dve.wait_ge(split_hi, KT * (j + 1) + k + 1)
                    cols = slice(OFF, OFF + W_OUT[j])
                    dve.tensor_tensor(h_lo[:, k, cols], g[:, k, 0:W_OUT[j]], h_hi[:, k, cols].bitcast(F32),
                                      ALU.subtract).then_inc(h_ready, 1)

            for m in range(KT):
                step(0, m, m % 2, w_st[:, m % 2] if m < KT - 2 else w1_eff[:, m - 6], m + 3)
                if m == KT - 1:
                    turn(0)
                    dve.wait_ge(acc_free, 2 + KT + 1)
                    dve.wait_ge(acc_part, KT + 1)
                    add_bp(slice(R, 2 * R), 0, slice(R, 2 * R), C_LOW2)
                for n, part in QUANT[0][m]:
                    quantise(n, part)
                if m == 0:
                    split_b()
            for m in range(KT - 2):
                step(1, m, m % 2, w1_eff[:, (m + 2) % SLOTS], m + KT + 3)
                for n, part in QUANT[1].get(m, ()):
                    quantise(n, part)
            step(1, 6, 0, w_st[:, 0], 2 * KT + 1)
            turn(1, 0, KT - 1)
            step(1, 7, 1, w_st[:, 1], 2 * KT + 2)
            turn(1, KT - 1, KT)
            labels()
            dve.wait_ge(a0_hd, 1)
            dve.tensor_tensor(a0_lo[:], a0_raw[:], a0_hi[:].bitcast(F32), ALU.subtract).then_inc(a0_done, 1)
            with dve.Fori(0, KT // 2 - 1) as i:
                for h in range(2):
                    m = i * 2 + h
                    step(2, m, h, w_st[:, h], m + (2 * KT + 3))
            dve.wait_ge(b3_hd, 1)
            dve.tensor_tensor(b3_lo[:], aux[:, :], b3_hi[:].bitcast(F32), ALU.subtract).then_inc(b3_done, 1)

            def x_turn(t, h, half, load):
                dve.wait_ge(x_in[h], 16 * QUARTERS * load)
                if not isinstance(t, int) or t:
                    dve.wait_ge(x_hd, t * 2 + (half - 1))
                    dve.wait_ge(x_split, t * 2 + (half - 1))
                dve.sem_inc(x_seen, 1)
                ks = slice(half * HALF, (half + 1) * HALF)
                dve.transpose(xt.rearrange("p k (c r) -> p c k r", r=Q)[:, :, ks].bitcast(U32),
                              x_st[:, h].rearrange("p (c k q) -> p c k q", c=QUARTERS, q=Q)[:, :, ks].bitcast(U32)
                              ).then_inc(x_tr, 1)

            def x_low(t, h, half):
                dve.wait_ge(x_hd, t * 2 + (half + 1))
                ks = slice(half * HALF, (half + 1) * HALF)
                dve.tensor_tensor(xt_lo[:, h, ks, :], xt[:, ks, :],
                                  xt_hi[:, h, ks, :].bitcast(F32), ALU.subtract).then_inc(x_split, 1)

            x_turn(0, 0, 0, 1)
            x_turn(0, 0, 1, 1)
            x_low(0, 0, 0)
            x_low(0, 0, 1)
            dve.wait_ge(low_hd, 1)
            dve.tensor_tensor(low_lo[:], g[:, :, C_LOW2:], low_hi[:].bitcast(F32), ALU.subtract).then_inc(low_done, 1)
            turn(2)
            dve.wait_ge(h_ready, 4 * KT)

            for lead in (R, 3 * R):
                rows = slice(lead, lead + R)
                dve.tensor_copy(c_hi[rows, :].rearrange("p (l c) -> p l c", l=LABELS),
                                ident[rows, rows].unsqueeze(1).to_broadcast([R, LABELS, R])).then_inc(vb_done, 1)
            dve.memset(c_lo[R:2 * R].bitcast(F32), 0.0).then_inc(vb_done, 1)

            def split_bp():
                dve.wait_ge(vb_hd, 2)
                dve.tensor_tensor(c_lo[0:R], bp[0:R, C_LOW2:C_ALL], c_hi[0:R].bitcast(F32), ALU.subtract).then_inc(vb_done, 1)
                dve.wait_ge(vb_hd, 3)
                dve.tensor_tensor(vb_lo[:], bp[:, 0:C_LOW2], vb_hi[0:2 * R].bitcast(F32),
                                  ALU.subtract).then_inc(vb_done, 1)

            def tile(t, b, h, finish, ahead):
                s = 1 - h
                if finish:
                    dve.wait_ge(main_done, t)
                    dve.tensor_copy(v_sb[:], v_columns(s).unsqueeze(1).to_broadcast([P, 2, 2 * R])).then_inc(v_out, 1)
                if ahead:
                    x_turn(t + 1, s, 0, b + 1 + h)
                    x_turn(t + 1, s, 1, b + 1 + h)
                if finish:
                    dve.wait_ge(v_hd, t)
                    dve.tensor_tensor(vt[2 * R:], aux[2 * R:, BANK:BANK + P], vt[2 * R:].bitcast(F32),
                                      ALU.subtract).then_inc(v_split, 1)
                if ahead:
                    x_low(t + 1, s, 0)
                if finish:
                    dve.wait_ge(m_hd, t)
                    dve.tensor_tensor(vm[2 * R:], aux[2 * R:, BANK + P:BANK + 2 * P], vm[2 * R:].bitcast(F32),
                                      ALU.subtract).then_inc(m_split, 1)
                    lg, top, idx, g0, g1 = (gate[:, 8 * n:8 * n + 8] for n in (0, 1, 2, 4, 5))
                    link.n = t * GLINKS + (base - GLINKS)
                    dve.wait_ge(r_done, t)
                    link(dve.tensor_tensor(lg, in_bank(s, s, C_LOGIT, C_LOW2), bias7[:, b - 1 + h, :], ALU.add))
                    dve.sem_inc(logits_seen, 1)
                    link(dve.max(top, lg))
                    dve.tensor_tensor(gate[:, 25:26], gate[:, 9:10], gate[:, 8:9], ALU.subtract).then_inc(d_ready, 1)
                    link(dve.max_index(top_i[:], top, lg))
                    link(dve.tensor_copy(idx[:, 0:2], top_i[:, 0:2]))
                    dve.wait_ge(e_ready, t)
                    link(dve.tensor_scalar(gate[:, 26:27], gate[:, 24:25], 1.0, 0.5, ALU.add, ALU.mult))
                    link(dve.reciprocal(gate[:, 27:28], gate[:, 26:27]))
                    link(dve.tensor_scalar(gate[:, 28:29], gate[:, 27:28], gate[:, 24:25], None, ALU.mult))
                    link(dve.tensor_scalar(g0, iota_f[:], idx[:, 0:1], gate[:, 27:28], ALU.is_equal, ALU.mult))
                    link(dve.tensor_scalar(g1, iota_f[:], idx[:, 1:2], gate[:, 28:29], ALU.is_equal, ALU.mult))
                    link(dve.tensor_tensor(g0, g0, g1, ALU.add))
                    dve.tensor_tensor(hg[:], in_bank(s, s, C_H, C_LOGIT).rearrange("p (e r) -> p e r", e=E),
                                      g0.unsqueeze(2).to_broadcast([P, E, RE]), ALU.mult).then_inc(hg_ready, 1)
                if not finish:
                    dve.wait_ge(acc_free, 2 + PASSES)
                    add_bp(slice(0, R), 1, slice(0, R), C_ALL)
                if ahead:
                    x_low(t + 1, s, 1)
                if not finish:
                    split_bp()
                if finish:
                    dve.wait_ge(g_hd, t)
                    dve.tensor_tensor(hgt_l[:], aux[:, BANK + 2 * P:BANK + 3 * P], hgt_h[:].bitcast(F32),
                                      ALU.subtract).then_inc(g_split, 1)
                    dve.wait_ge(o_done, t)
                    dve.wait_ge(out_done[s], (b + h) * 16)
                    where, c0, c1 = list(in_banks(s, s, 0, D))[2]
                    dve.tensor_copy(out_sb[:, s, c0:c1], where).then_inc(o_dve, 1)

            base = link.n

            tile_schedule(dve, tile)

        @block.tensor
        def _(pe):
            def turn_tile(dst, src):
                return pe.transpose(dst, src, ident[0:src.shape[0], 0:src.shape[0]])

            def pass_tile(j, k, slot, pairs):
                pe.wait_ge(h_ready, KT * j + k + 1)
                for n, (a, b) in enumerate(pairs):
                    for bank, (c0, c1) in enumerate(thirds(W_IN[j])):
                        last = pe.matmul(acc[0:a.shape[-1], slot, bank * BANK:bank * BANK + c1 - c0],
                                         a[:, k, :], b[:, k, OFF + c0:OFF + c1], start=(k == 0 and n == 0),
                                         stop=(k == KT - 1 and n == len(pairs) - 1), skip_group_check=True)
                last.then_inc(h_used if k < KT - 1 else acc_done, 1)

            def turn_w3(k):
                pe.wait_ge(w3_eye, k + 1)
                if k >= 2:
                    pe.wait_ge(h_ready, k - 1)
                for n in range(KT):
                    last = turn_tile(w3_at(k)[:, n * P:(n + 1) * P], g[:, n, k * P:(k + 1) * P])
                last.then_inc(w3_t, 1)

            pe.wait_ge(made, 2)
            turn_w3(0)
            pe.wait_ge(a3_in, 32)
            for bank, (k0, k1) in enumerate(a3_tiles):
                for k in range(k0, k1):
                    at = a3_at(bank, k0, k1)[:, k - k0]
                    turn_tile(at[:, 0:ER], w1_eff[:, 0, k, :])
                    last = turn_tile(at[:, ER:NR], w1_eff[0:E, 1, k, :])
            last.then_inc(a3_t, 1)
            for k in range(KT):
                if k + 1 < KT:
                    turn_w3(k + 1)
                if k == 0:
                    pe.wait_ge(w_split, 1)
                    pe.wait_ge(a3_done, len(a3_tiles))
                if k == KT - 1:
                    pe.wait_ge(tables_in, 64)
                    pe.wait_ge(h_ready, KT - 1)
                    b1 = w1_eff[:, 2, 0:HALF].rearrange("p k i -> p (k i)").rearrange("p (k r) -> p k r", r=R1)
                    for n in range(KT):
                        last = turn_tile(aux[0:R1, n * P:(n + 1) * P], b1[:, n, :])
                    last.then_inc(b1_t, 1)
                pass_tile(0, k, 0, ((w_hi[:, 0], h_hi), (w_hi[:, 0], h_lo), (w_lo[:, 0], h_hi)))
            def delta(m):
                pe.wait_ge(aux_free, m + 1)
                for k in range(KT):
                    last = pe.matmul(aux[:, k * P:(k + 1) * P], b1t[:, k * P:(k + 1) * P],
                                     a1[:, bass.ds(m * P, P)], start=True, stop=True)
                last.then_inc(ld_done, 1)

            def one_pass(j, slot, w_h, w_l):
                for k in range(KT):
                    pass_tile(j, k, slot, ((w_h, h_hi), (w_h, h_lo), (w_l, h_hi)))

            def small_pass(j, slot, both):
                for k in range(KT):
                    pass_tile(j, k, slot, ((both, h_hi), (both[:, :, 0:R], h_lo)))

            def step(j, m, h):
                pe.wait_ge(w_split, m + (KT * j + 1))
                pe.wait_ge(acc_free, m + (STEP0[j] + 1))
                one_pass(j, (STEP0[j] + h) % 2, w_hi[:, h], w_lo[:, h])

            for m in range(1, KT):
                if (n := FIRST_PART[0].get(m - 1)) is not None:
                    delta(n)
                step(0, m, m % 2)
            pe.wait_ge(b_split, 2)
            pe.wait_ge(acc_free, KT + 1)
            small_pass(0, 0, b2s)
            for m in range(KT):
                if (n := FIRST_PART[1].get(m - 1)) is not None:
                    delta(n)
                if m == 1:
                    pe.wait_ge(bp_added, 1)
                step(1, m, m % 2)
            with pe.Fori(0, KT // 2 - 1) as i:
                for h in range(2):
                    step(2, i * 2 + h, h)
            pe.wait_ge(b3_in, 16 * E)
            pe.wait_ge(aux_free, KT + 1)
            for k in range(KT):
                last = turn_tile(aux[:, k * P:(k + 1) * P], b3_raw[:, k].rearrange("p e r -> p (e r)"))
            last.then_inc(b3_t, 1)
            for m in (6, 7):
                step(2, m, m % 2)

            pe.wait_ge(acc_free, PASSES)
            small_pass(2, 1, b0s)

            def three(dst, a, b, start=False, stop=False):
                (ah, al), (bh, bl) = a, b
                for n, (p, q) in enumerate(((ah, bh), (ah, bl), (al, bh))):
                    last = pe.matmul(dst, p, q, start=start and n == 0, stop=stop and n == 2, skip_group_check=True)
                return last

            def tile(t, b, h, finish, ahead):
                s = 1 - h

                def products(k, slot, banks):
                    for n, (a, b) in enumerate(((xt_hi, h_hi), (xt_hi, h_lo), (xt_lo, h_hi))):
                        for bank in banks:
                            c0 = (0, OFF)[slot] + bank * PART
                            last = pe.matmul(acc[:, slot, bank * BANK:bank * BANK + PART],
                                             a[:, slot, k, :], b[:, k, c0:c0 + PART],
                                             start=(k == 0 and n == 0), stop=False, skip_group_check=True)
                    return last

                if ahead is not None:
                    pe.wait_ge(x_split, t * 2 + 2)
                    if finish:
                        if isinstance(t, int) and t == 1:
                            pe.wait_ge(bp_added, 2)
                        if not isinstance(t, int) or t >= 2:
                            pe.wait_ge(o_act[0], t - 1)
                            pe.wait_ge(o_act[1], t - 1)
                            pe.wait_ge(o_dve, t - 1)
                            pe.wait_ge(hg_ready, t - 1)
                    pe.wait_ge(sel_ready, t * SELS + SELS)
                for k in range(KT):
                    if ahead is not None:
                        if not finish:
                            pe.wait_ge(h_ready, 3 * KT + k + 1)
                        last = products(k, h, (0, 1, 2) if ahead else (0, 2))
                    else:
                        products(k, s, (1,))
                    if finish and k == 0:
                        pe.wait_ge(v_out, t)
                        turn_tile(aux[:, BANK:BANK + P], v_sb[:].rearrange("p u c -> p (u c)")).then_inc(v_tr, 1)
                    if finish and k == 2:
                        pe.wait_ge(v_split, t)
                        pe.wait_ge(tsel_ready, t * 2)
                        mixed = aux[:, BANK + P:BANK + 2 * P]
                        pe.matmul(mixed, tsel_h[:, s], vt[:], start=True, stop=False, skip_group_check=True)
                        pe.matmul(mixed, tsel_l[:, s], vt[0:2 * R], start=False, stop=True,
                                  skip_group_check=True).then_inc(mix_done, 1)
                    if finish and k == 3:
                        if isinstance(t, int) and t == 1:
                            pe.wait_ge(vb_hd, 4)
                            pe.wait_ge(vb_done, 5)
                        pe.wait_ge(m_split, t)
                        for bank, (where, c0, c1) in reversed(list(enumerate(in_banks(s, s, 0, C_LOW2)))):
                            pe.matmul(where, vm[:], vb_hi[:, c0:c1], start=False, stop=False, skip_group_check=True)
                            last = pe.matmul(where, vm[0:2 * R], vb_lo[:, c0:c1], start=False, stop=(bank == 2),
                                             skip_group_check=True)
                            if bank == 2:
                                last.then_inc(r_done, 1)
                    if finish and k == 5:
                        pe.wait_ge(hg_ready, t)
                        turn_tile(aux[:, BANK + 2 * P:BANK + 3 * P],
                                  hg[:].rearrange("p e r -> p (e r)")).then_inc(g_tr, 1)
                    if finish and k == (6 if ahead is not None else 7):
                        pe.wait_ge(g_split, t)
                        for where, c0, c1 in in_banks(s, s, 0, D):
                            done = three(where, (hgt_h[:], hgt_l[:]), (b3_hi[:, c0:c1], b3_lo[:, c0:c1]),
                                         stop=True)
                        done.then_inc(o_done, 1)
                    if ahead is not None and k == KT - 1:
                        last.then_inc(main_done, 1)

            pe.wait_ge(b3_done, 1)
            tile_schedule(pe, tile)
    return nc


_INS = ['x', 'itok_B_0_4', 'condB_codebook', 'itok_B_0_2', 'itok_B_0_7', 'L0_cond_weight', 'L0_cond_lora_A',
        'L0_cond_lora_B_w', 'L1_cond_weight', 'L1_cond_scale_log', 'L1_cond_lora_A', 'L1_cond_lora_B',
        'L2_cond_W', 'L2_cond_lora_A', 'L2_cond_lora_B_w', 'L3_cond_W', 'L3_cond_Wr', 'L3_cond_A', 'L3_cond_B']


def kernel(**inputs):
    import numpy as _np
    import concourse.bacc as _bacc
    from concourse import mybir as _mybir
    from concourse.bass_utils import run_bass_kernel_spmd as _run

    nc = _bacc.Bacc("TRN2", target_bir_lowering=False, num_devices=1)
    arrays, args = {}, []
    for name in _INS:
        a = _np.ascontiguousarray(inputs[name])
        arrays[f"in_{name}_dram"] = a
        args.append(nc.dram_tensor(f"in_{name}_dram", a.shape, _mybir.dt.from_np(a.dtype), kind="ExternalInput").ap())
    shape = inputs['x'].shape
    args.append(nc.dram_tensor("out_0_dram", shape, _mybir.dt.float32, kind="ExternalOutput").ap())
    build(nc, *args)
    r = _run(nc, [arrays], core_ids=[0])
    return r.results[0]["out_0_dram"]
```
